# Optimizing a Trainium2 kernel written in Bass

```python
import numpy as np
import jax
import jax.numpy as jnp

def _softmax(x, axis=-1):
    return jax.nn.softmax(x, axis=axis)

def _gelu(x):
    return jax.nn.gelu(x, approximate=True)

def _silu(x):
    return jax.nn.silu(x)

def _sigmoid(x):
    return jax.nn.sigmoid(x)

def _layernorm(x, axis=-1, eps=1e-05):
    m = jnp.mean(x, axis=axis, keepdims=True)
    v = jnp.var(x, axis=axis, keepdims=True)
    return (x - m) / jnp.sqrt(v + eps)

def _scatter_add(tgt, idx, src, axis=0):
    return tgt.at[idx].add(src)

def _segment_sum(src, seg, n):
    return jax.ops.segment_sum(src, seg, n)
kernel_name = 'mk_adaln_d1_jaxref_r2_f84720'

def setup_inputs(seed: int=0):
    np.random.seed(seed)
    _w = jnp.asarray

    def _L0_attn_setup():
        import jax, jax.numpy as jnp
        import numpy as np
        EPS_FEAT = 1.0 + 0.0001
        EPS_DEN = 1e-06

        def _linear_attention(x, W_qkv, b_qkv, W_out, b_out, num_heads=16):
            B, L, D = x.shape
            H = num_heads
            E = D // H
            qkv = x @ W_qkv + b_qkv
            q, k, v = jnp.split(qkv, 3, axis=-1)
            q = q.reshape(B, L, H, E)
            k = k.reshape(B, L, H, E)
            v = v.reshape(B, L, H, E)
            q = jax.nn.elu(q * E ** (-0.5)) + EPS_FEAT
            k = jax.nn.elu(k) + EPS_FEAT
            qL = jnp.moveaxis(q, 1, 0)
            kL = jnp.moveaxis(k, 1, 0)
            vL = jnp.moveaxis(v, 1, 0)
            kv0 = jnp.zeros((B, H, E, E), dtype=x.dtype)
            ks0 = jnp.zeros((B, H, E), dtype=x.dtype)

            def step(carry, qkv_t):
                kv_s, k_s = carry
                q_t, k_t, v_t = qkv_t
                kv_s = kv_s + jnp.einsum('bhe,bhf->bhef', k_t, v_t)
                k_s = k_s + k_t
                num = jnp.einsum('bhe,bhef->bhf', q_t, kv_s)
                den = jnp.einsum('bhe,bhe->bh', q_t, k_s)[..., None] + EPS_DEN
                return ((kv_s, k_s), num / den)
            _, out = jax.lax.scan(step, (kv0, ks0), (qL, kL, vL))
            out = jnp.moveaxis(out, 0, 1).reshape(B, L, D)
            return out @ W_out + b_out
        key = jax.random.key(seed)
        k1, k2, k3 = jax.random.split(key, 3)
        B, L, D = (4, 2048, 512)
        x = jax.random.normal(k1, (B, L, D), dtype=jnp.float32)
        W_qkv = jax.random.normal(k2, (D, 3 * D), dtype=jnp.float32) / np.sqrt(D)
        b_qkv = jnp.zeros((3 * D,), dtype=jnp.float32)
        W_out = jax.random.normal(k3, (D, D), dtype=jnp.float32) / np.sqrt(D)
        b_out = jnp.zeros((D,), dtype=jnp.float32)
        return {'x': x, 'W_qkv': W_qkv, 'b_qkv': b_qkv, 'W_out': W_out, 'b_out': b_out}
    _L0_attn_in = _L0_attn_setup()

    def _L0_ffn_setup():
        import jax, jax.numpy as jnp
        import numpy as np
        DIM = 512
        HIDDEN = 1536
        SCALE = 1.0 / 127.0

        def _dequant(w_int, dtype):
            return w_int.astype(dtype) * jnp.asarray(SCALE, dtype)
        key = jax.random.key(seed)
        k_x, k_g, k_u, k_d = jax.random.split(key, 4)
        x = jax.random.normal(k_x, (4, 1024, DIM), dtype=jnp.float32)
        w_gate = jax.random.randint(k_g, (HIDDEN, DIM), -127, 128, dtype=jnp.int32)
        w_up = jax.random.randint(k_u, (HIDDEN, DIM), -127, 128, dtype=jnp.int32)
        w_down = jax.random.randint(k_d, (DIM, HIDDEN), -127, 128, dtype=jnp.int32)
        return {'x': x, 'w_gate': w_gate, 'w_up': w_up, 'w_down': w_down}
    _L0_ffn_in = _L0_ffn_setup()
    _L0_c = _w((lambda *s: np.random.randn(*s).astype(np.float32) * 0.05)(1, 512))
    _L0_wmod = _w((lambda *s: np.random.randn(*s).astype(np.float32) * 0.05)(512, 6 * 512) * 512 ** (-0.5))
    _d = {'L0_attn_x': _L0_attn_in['x'], 'L0_attn_W_qkv': _L0_attn_in['W_qkv'], 'L0_attn_b_qkv': _L0_attn_in['b_qkv'], 'L0_attn_W_out': _L0_attn_in['W_out'], 'L0_attn_b_out': _L0_attn_in['b_out'], 'L0_ffn_w_gate': _L0_ffn_in['w_gate'], 'L0_ffn_w_up': _L0_ffn_in['w_up'], 'L0_ffn_w_down': _L0_ffn_in['w_down'], 'L0_c': _L0_c, 'L0_wmod': _L0_wmod}
    _x0 = _d['L0_attn_x']
    _d['L0_attn_x'] = jax.random.normal(jax.random.fold_in(jax.random.key(seed), 1), (1, 8192, 512), dtype=_x0.dtype)
    del _x0
    return _d

def reference(L0_attn_x, L0_attn_W_qkv, L0_attn_b_qkv, L0_attn_W_out, L0_attn_b_out, L0_ffn_w_gate, L0_ffn_w_up, L0_ffn_w_down, L0_c, L0_wmod):

    def _L0_attn_ref(x, W_qkv, b_qkv, W_out, b_out):
        import jax, jax.numpy as jnp
        import numpy as np
        EPS_FEAT = 1.0 + 0.0001
        EPS_DEN = 1e-06

        def _linear_attention(x, W_qkv, b_qkv, W_out, b_out, num_heads=16):
            B, L, D = x.shape
            H = num_heads
            E = D // H
            qkv = x @ W_qkv + b_qkv
            q, k, v = jnp.split(qkv, 3, axis=-1)
            q = q.reshape(B, L, H, E)
            k = k.reshape(B, L, H, E)
            v = v.reshape(B, L, H, E)
            q = jax.nn.elu(q * E ** (-0.5)) + EPS_FEAT
            k = jax.nn.elu(k) + EPS_FEAT
            qL = jnp.moveaxis(q, 1, 0)
            kL = jnp.moveaxis(k, 1, 0)
            vL = jnp.moveaxis(v, 1, 0)
            kv0 = jnp.zeros((B, H, E, E), dtype=x.dtype)
            ks0 = jnp.zeros((B, H, E), dtype=x.dtype)

            def step(carry, qkv_t):
                kv_s, k_s = carry
                q_t, k_t, v_t = qkv_t
                kv_s = kv_s + jnp.einsum('bhe,bhf->bhef', k_t, v_t)
                k_s = k_s + k_t
                num = jnp.einsum('bhe,bhef->bhf', q_t, kv_s)
                den = jnp.einsum('bhe,bhe->bh', q_t, k_s)[..., None] + EPS_DEN
                return ((kv_s, k_s), num / den)
            _, out = jax.lax.scan(step, (kv0, ks0), (qL, kL, vL))
            out = jnp.moveaxis(out, 0, 1).reshape(B, L, D)
            return out @ W_out + b_out
        return _linear_attention(x, W_qkv, b_qkv, W_out, b_out)

    def _L0_ffn_ref(x, w_gate, w_up, w_down):
        import jax, jax.numpy as jnp
        import numpy as np
        DIM = 512
        HIDDEN = 1536
        SCALE = 1.0 / 127.0

        def _dequant(w_int, dtype):
            return w_int.astype(dtype) * jnp.asarray(SCALE, dtype)
        wg = _dequant(w_gate, x.dtype)
        wu = _dequant(w_up, x.dtype)
        wd = _dequant(w_down, x.dtype)
        gate = jnp.einsum('bsd,hd->bsh', x, wg)
        up = jnp.einsum('bsd,hd->bsh', x, wu)
        h = jax.nn.silu(gate) * up
        return jnp.einsum('bsh,dh->bsd', h, wd)
    x = L0_attn_x
    mod = (_silu(L0_c) @ L0_wmod).reshape(L0_c.shape[0], 6, 1, -1)
    sa, ca, ga, sb, cb, gb = (mod[:, 0], mod[:, 1], mod[:, 2], mod[:, 3], mod[:, 4], mod[:, 5])
    ga = (2 * (ga >= 0) - 1) * jnp.maximum(jnp.abs(ga), 0.25)
    gb = (2 * (gb >= 0) - 1) * jnp.maximum(jnp.abs(gb), 0.25)
    h = _layernorm(x, axis=-1) * (1 + ca) + sa
    x = x + ga * _L0_attn_ref(h, L0_attn_W_qkv, L0_attn_b_qkv, L0_attn_W_out, L0_attn_b_out)
    h = _layernorm(x, axis=-1) * (1 + cb) + sb
    x = x + gb * _L0_ffn_ref(h, L0_ffn_w_gate, L0_ffn_w_up, L0_ffn_w_down)
    return x

_drawn_inputs = setup_inputs


def setup_inputs(seed=0):
    import zlib

    import numpy as np

    out = dict(_drawn_inputs(seed))
    spreads = {'L0_attn_b_qkv': (0.0, 0.1), 'L0_attn_b_out': (0.0, 0.1)}
    factors = {'L0_attn_W_qkv': 4.855}
    for name, (base, spread) in spreads.items():
        noise = np.random.default_rng([zlib.crc32(name.encode()), seed]).standard_normal(out[name].shape)
        drawn = base * np.exp(spread * noise) if base else spread * noise
        out[name] = jnp.asarray(drawn.astype(out[name].dtype))
    for name, factor in factors.items():
        out[name] = (out[name] * factor).astype(out[name].dtype)
    return out
```

```python
from contextlib import ExitStack

import numpy as np

import concourse.bass as bass
from concourse import mybir

F32 = mybir.dt.float32
F32R = mybir.dt.float32r
I32 = mybir.dt.int32
ALU = mybir.AluOpType
ACT = mybir.ActivationFunctionType
AX = mybir.AxisListType

P = 128
L = 8192
D = 512
HID = 1536
E = 32
C = D // P
HB = HID // P
HPC = P // E
GT = 4
GN = GT * P
NG = L // GN
UNITS = 3 * C
EPS_LN = 1e-5
EPS_FEAT = 1e-4
EPS_DEN = 1e-6
Q_SCALE = float(E) ** -0.5
W_SCALE = float(np.float32(1.0 / 127.0))


def wait(eng, sem, value):
    if not isinstance(value, int) or value > 0:
        eng.wait_ge(sem, value)


def groups(eng, first, last, body):
    for g in range(first):
        body(g, g % 2)
    with eng.Fori(first // 2, last // 2) as pair:
        for parity in range(2):
            body(pair * 2 + parity, parity)
    for g in range(last, NG):
        body(g, g % 2)


def build(nc, x, w_qkv, b_qkv, w_out, b_out, w_gate_t, w_up_t, w_down_t, c_vec, w_mod, out):
    top = ExitStack()
    with top:
        def sem(name):
            return top.enter_context(nc.semaphore(name))

        def sbuf(stack, name, shape, dt=F32):
            return stack.enter_context(nc.sbuf_tensor(name, shape, dt))

        def psum(stack, name, shape):
            return stack.enter_context(nc.psum_tensor(name, shape, F32))

        x_mid = nc.dram_tensor("x_mid", (L, D), F32, kind="Internal").ap()

        ident = sbuf(top, "ident", [P, P])
        gb_row = sbuf(top, "gb_row", [P, D])
        mod_col = sbuf(top, "mod_col", [P, 4, C])
        half_neg = sbuf(top, "half_neg", [P, GT])
        SA, CA, SB, CB = range(4)

        with ExitStack() as attn:
            w_hi = sbuf(attn, "w_hi", [P, C, 4 * D], F32R)
            w_lo = sbuf(attn, "w_lo", [P, C, 4 * D], F32R)
            ga_row = sbuf(attn, "ga_row", [P, D])
            gabo_row = sbuf(attn, "gabo_row", [P, D])
            bv_row = sbuf(attn, "bv_row", [P, D])
            qk_bias = sbuf(attn, "qk_bias", [P, 2, C])
            causal = sbuf(attn, "causal", [P, P])
            head_diag = sbuf(attn, "head_diag", [P, P])
            head_ones = sbuf(attn, "head_ones", [P, P], F32R)
            setup(nc, sem, sbuf, psum, ident, gb_row, mod_col, half_neg, w_hi, w_lo, ga_row, gabo_row,
                  bv_row, qk_bias, causal, head_diag, head_ones, w_qkv, b_qkv, w_out, b_out, c_vec, w_mod)
            attention(nc, sem, sbuf, psum, ident, mod_col[:, CA, :], half_neg, w_hi, w_lo, ga_row, gabo_row,
                      bv_row, qk_bias, causal, head_diag, head_ones, x, x_mid)
        with ExitStack() as ffn:
            wg = sbuf(ffn, "wg", [P, C, HID], F32R)
            wu = sbuf(ffn, "wu", [P, C, HID], F32R)
            wd = sbuf(ffn, "wd", [P, HB, D], F32R)
            gu_bias = sbuf(ffn, "gu_bias", [P, 2, HB])
            wide = sbuf(ffn, "wide", [1, 1], I32)
            load_ffn(nc, sem, sbuf, psum, ident, mod_col[:, SB, :], wg, wu, wd, gu_bias, wide,
                     w_gate_t, w_up_t, w_down_t)
            feed_forward(nc, sem, sbuf, psum, ident, mod_col[:, CB, :], half_neg, wg, wu, wd, gu_bias, wide,
                         gb_row, x_mid, out)


def setup(nc, sem, sbuf, psum, ident, gb_row, mod_col, half_neg, w_hi, w_lo, ga_row, gabo_row,
          bv_row, qk_bias, causal, head_diag, head_ones, w_qkv, b_qkv, w_out, b_out, c_vec, w_mod):
    SAm, CAm, GAm, SBm, CBm, GBm = range(6)
    with ExitStack() as s:
        w_raw = sbuf(s, "w_raw", [P, C, 4 * D])
        wm = sbuf(s, "wm", [P, C, 6 * D])
        mod_row = sbuf(s, "mod_row", [P, 6, D])
        b_row = sbuf(s, "b_row", [P, 4 * D])
        c_col = sbuf(s, "c_col", [P, C])
        c_exp = sbuf(s, "c_exp", [P, C])
        c_bc = sbuf(s, "c_bc", [P, C, P])
        sa_bc = sbuf(s, "sa_bc", [P, C, P])
        ones = sbuf(s, "ones", [P, P])
        sign = sbuf(s, "sign", [P, D])
        size = sbuf(s, "size", [P, D])
        banks = psum(s, "setup_banks", [P, 8, 512])

        c_in, w_in, b_in = sem("c_in"), sem("w_in"), sem("b_in")
        wm_in = [sem(f"wm_in{m}") for m in range(6)]
        const_done, pool_chain, c_neg_exp = sem("const_done"), sem("pool_chain"), sem("c_neg_exp")
        dve_chain, act_chain = sem("setup_dve_chain"), sem("setup_act_chain")
        c_ready, mod_mm, mod_ev, col_tp, col_ev = (sem("c_ready"), sem("mod_mm"), sem("mod_ev"), sem("col_tp"),
                                                   sem("col_ev"))
        q_scaled, sa_ready, hi_done, bias_mm, bias_ev, qk_tp = (sem("q_scaled"), sem("sa_ready"), sem("hi_done"),
                                                                sem("bias_mm"), sem("bias_ev"), sem("qk_tp"))

        with nc.Block() as block:
            @block.sync
            def _(sp):
                sp.dma_start(c_col[:, :], c_vec).then_inc(c_in, 16)
                for m in (SAm, CAm, GAm, SBm, CBm, GBm):
                    sp.dma_start(wm[:, :, m * D:(m + 1) * D],
                                 w_mod[:, m * D:(m + 1) * D].rearrange("(c p) n -> p c n", p=P)).then_inc(wm_in[m], 16)

            @block.gpsimd
            def _(pool):
                pool.memset(ident[:, :], 0.0).then_inc(pool_chain, 1)
                pool.memset(causal[:, :], 1.0).then_inc(pool_chain, 1)
                pool.wait_ge(pool_chain, 2)
                pool.affine_select(out=ident[:, :], in_=ident[:, :], compare_op=ALU.not_equal, fill=1.0,
                                   base=0, pattern=[[-1, P]], channel_multiplier=1).then_inc(const_done, 1)
                pool.affine_select(out=causal[:, :], in_=causal[:, :], compare_op=ALU.is_ge, fill=0.0,
                                   base=0, pattern=[[1, P]], channel_multiplier=-1).then_inc(const_done, 1)

            @block.scalar
            def _(act):
                act.dma_start(w_raw[:, :, 0:3 * D], w_qkv.rearrange("(c p) n -> p c n", p=P)).then_inc(w_in, 16)
                act.dma_start(w_raw[:, :, 3 * D:4 * D], w_out.rearrange("(c p) n -> p c n", p=P)).then_inc(w_in, 16)
                act.dma_start(b_row[:, 0:3 * D], b_qkv.rearrange("(a n) -> a n", a=1).broadcast_to([P, 3 * D])).then_inc(b_in, 16)
                act.dma_start(b_row[:, 3 * D:4 * D], b_out.rearrange("(a n) -> a n", a=1).broadcast_to([P, D])).then_inc(b_in, 16)
                act.wait_ge(c_in, 16)
                act.activation(c_exp[:, :], c_col[:, :], ACT.Exp, scale=-1.0).then_inc(c_neg_exp, 1)
                act.wait_ge(w_in, 32)
                act.wait_ge(q_scaled, 1)
                for k in range(C):
                    act.activation(w_hi[:, k, :], w_raw[:, k, :], ACT.Copy).then_inc(hi_done, 1)

            @block.vector
            def _(dve):
                chain = [0]

                def link(ins):
                    chain[0] += 1
                    ins.then_inc(dve_chain, 1)
                    dve.wait_ge(dve_chain, chain[0])

                dve.memset(ones[:, :], 1.0)
                dve.memset(half_neg[:, :], -0.5)
                link(dve.memset(head_diag[:, :], 0.0))
                for h in range(HPC):
                    ins = dve.memset(head_diag[h * E:(h + 1) * E, h * E:(h + 1) * E], 1.0)
                link(ins)
                dve.tensor_copy(head_ones[:, :], head_diag[:, :])
                dve.wait_ge(c_neg_exp, 1)
                link(dve.tensor_scalar(c_exp[:, :], c_exp[:, :], 1.0, None, ALU.add))
                link(dve.reciprocal(c_exp[:, :], c_exp[:, :]))
                link(dve.tensor_tensor(out=c_col[:, :], in0=c_col[:, :], in1=c_exp[:, :], op=ALU.mult))
                for k in range(C):
                    ins = dve.tensor_scalar(c_bc[:, k, :], ones[:, :], c_col[:, k:k + 1], None, ALU.mult)
                ins.then_inc(c_ready, 1)
                dve.wait_ge(w_in, 32)
                dve.tensor_scalar(w_raw[:, :, 0:D], w_raw[:, :, 0:D], Q_SCALE, None, ALU.mult).then_inc(q_scaled, 1)
                dve.wait_ge(b_in, 32)
                link(dve.tensor_scalar(b_row[:, 0:D], b_row[:, 0:D], Q_SCALE, None, ALU.mult))
                for m in range(6):
                    dve.wait_ge(mod_mm, m + 1)
                    dve.tensor_copy(mod_row[:, m, :], banks[:, m, :]).then_inc(mod_ev, 1)
                for n, m in enumerate((SAm, CAm, SBm, CBm)):
                    dve.wait_ge(col_tp, n + 1)
                    if n % 2:
                        dve.tensor_scalar(mod_col[:, n, :], banks[:, n, 0:D:P], 1.0, None, ALU.add).then_inc(col_ev, 1)
                    else:
                        dve.tensor_copy(mod_col[:, n, :], banks[:, n, 0:D:P]).then_inc(col_ev, 1)
                dve.wait_ge(col_ev, 4)
                for k in range(C):
                    ins = dve.tensor_scalar(sa_bc[:, k, :], ones[:, :], mod_col[:, 0, k:k + 1], None, ALU.mult)
                ins.then_inc(sa_ready, 1)
                dve.wait_ge(mod_ev, 6)
                for m, row in ((GAm, ga_row), (GBm, gb_row)):
                    g = mod_row[:, m, :]
                    link(dve.tensor_scalar(sign[:, :], g, 0.0, 2.0, ALU.is_ge, ALU.mult))
                    link(dve.tensor_scalar(sign[:, :], sign[:, :], -1.0, None, ALU.add))
                    link(dve.tensor_scalar(size[:, :], g, -1.0, 0.25, ALU.mult, ALU.max))
                    link(dve.tensor_tensor(out=size[:, :], in0=size[:, :], in1=g, op=ALU.max))
                    link(dve.tensor_tensor(out=row[:, :], in0=sign[:, :], in1=size[:, :], op=ALU.mult))
                link(dve.tensor_scalar(gb_row[:, :], gb_row[:, :], W_SCALE, W_SCALE, ALU.mult, ALU.mult))
                dve.tensor_tensor(out=gabo_row[:, :], in0=ga_row[:, :], in1=b_row[:, 3 * D:4 * D], op=ALU.mult)
                for k in range(C):
                    dve.wait_ge(hi_done, k + 1)
                    dve.tensor_tensor(out=w_lo[:, k, :], in0=w_raw[:, k, :], in1=w_hi[:, k, :].bitcast(F32),
                                      op=ALU.subtract)
                for n in range(3):
                    dve.wait_ge(bias_mm, n + 1)
                    row = b_row[:, n * D:(n + 1) * D] if n < 2 else bv_row[:, :]
                    dve.tensor_tensor(out=row, in0=banks[:, 4 + n, :], in1=b_row[:, n * D:(n + 1) * D],
                                      op=ALU.add).then_inc(bias_ev, 1)
                for n in range(2):
                    dve.wait_ge(qk_tp, n + 1)
                    ins = dve.tensor_copy(qk_bias[:, n, :], banks[:, n, 0:D:P])

            @block.tensor
            def _(pe):
                pe.wait_ge(c_ready, 1)
                for m in range(6):
                    pe.wait_ge(wm_in[m], 16)
                    for k in range(C):
                        mm = pe.matmul(banks[:, m, :], c_bc[:, k, :], wm[:, k, m * D:(m + 1) * D],
                                       start=(k == 0), stop=(k == C - 1))
                    mm.then_inc(mod_mm, 1)
                pe.wait_ge(const_done, 2)
                pe.wait_ge(mod_ev, 6)
                for n, m in enumerate((SAm, CAm, SBm, CBm)):
                    for k in range(C):
                        mm = pe.transpose(banks[:, n, k * P:(k + 1) * P], mod_row[:, m, k * P:(k + 1) * P], ident[:, :])
                    mm.then_inc(col_tp, 1)
                pe.wait_ge(sa_ready, 1)
                pe.wait_ge(q_scaled, 1)
                for n in range(3):
                    for k in range(C):
                        mm = pe.matmul(banks[:, 4 + n, :], sa_bc[:, k, :], w_raw[:, k, n * D:(n + 1) * D],
                                       start=(k == 0), stop=(k == C - 1))
                    mm.then_inc(bias_mm, 1)
                for n in range(2):
                    pe.wait_ge(bias_ev, n + 1)
                    for k in range(C):
                        mm = pe.transpose(banks[:, n, k * P:(k + 1) * P], b_row[:, n * D + k * P:n * D + (k + 1) * P],
                                          ident[:, :])
                    mm.then_inc(qk_tp, 1)


def attention(nc, sem, sbuf, psum, ident, scale_col, half_neg, w_hi, w_lo, ga_row, gabo_row,
              bv_row, qk_bias, causal, head_diag, head_ones, x, x_mid):
    WQ, WK, WV, WO = 0, D, 2 * D, 3 * D
    with ExitStack() as s:
        xg = sbuf(s, "xg", [P, GT, D])
        stats = sbuf(s, "stats", [P, GT, 6])
        mean_var = sbuf(s, "mean_var", [P, GT, 2])
        var_eps = sbuf(s, "var_eps", [P, GT])
        rstd = sbuf(s, "rstd", [P, GT])
        xt_hi = sbuf(s, "xt_hi", [P, C, GN], F32R)
        xt_lo = sbuf(s, "xt_lo", [P, C, GN], F32R)
        z_exp = sbuf(s, "z_exp", [P, 2, GN])
        z_relu = sbuf(s, "z_relu", [P, 2, GN])
        qt = [sbuf(s, f"qt{i}", [P, C, GN]) for i in range(2)]
        kt = [sbuf(s, f"kt{i}", [P, C, GN]) for i in range(2)]
        v = [sbuf(s, f"v{i}", [P, GT, D]) for i in range(2)]
        k_sum = sbuf(s, "k_sum", [P, C, GN])
        prod = sbuf(s, "prod", [P, GN])
        prod_hi = sbuf(s, "prod_hi", [P, GN], F32R)
        prod_lo = sbuf(s, "prod_lo", [P, GN], F32R)
        r_den = [sbuf(s, f"r_den{i}", [P, C, GN]) for i in range(2)]
        q_diag = sbuf(s, "q_diag", [P, C, HPC, P])
        probs = sbuf(s, "probs", [P, C, HPC * P])
        kv_diag = sbuf(s, "kv_diag", [P, C, P])
        k_tok = sbuf(s, "k_tok", [P, 2, D])
        a_t = sbuf(s, "a_t", [P, D])
        a_hi = sbuf(s, "a_hi", [P, D], F32R)
        a_lo = sbuf(s, "a_lo", [P, D], F32R)
        x_res = sbuf(s, "x_res", [P, 2, D])
        y = sbuf(s, "y", [P, 2, D])
        pj = psum(s, "pj", [P, 2, 512])
        sc = psum(s, "sc", [P, 2, 512])
        num = psum(s, "num", [P, 512])
        state = psum(s, "state", [P, 512])
        den_tp = psum(s, "den_tp", [P, 512])
        kt_op = psum(s, "kt_op", [P, 512])

        init_done, pool_passed, dve_passed = sem("init_done"), sem("pool_passed"), sem("dve_passed")
        x_in, xr_in, y_out = sem("x_in"), [sem(f"xr_in{i}") for i in range(2)], [sem(f"y_out{i}") for i in range(2)]
        ln_chain, var_ready, rstd_ready, xn_ready = sem("ln_chain"), sem("var_ready"), sem("rstd_ready"), sem("xn_ready")
        xt_ps, xt_hi_done, xt_lo_done = sem("xt_ps"), sem("xt_hi_done"), sem("xt_lo_done")
        pj_ready, exp_ready, relu_ready, emin_ready, phi_ready = (sem("pj_ready"), sem("exp_ready"), sem("relu_ready"),
                                                                  sem("emin_ready"), sem("phi_ready"))
        v_ready, ksum_ready, prod_ready, prod_hi_ready, prod_lo_ready = (
            sem("v_ready"), sem("ksum_ready"), sem("prod_ready"), sem("prod_hi_ready"), sem("prod_lo_ready"))
        den_ps, den_ready, rden_ready = sem("den_ps"), sem("den_ready"), sem("rden_ready")
        qdiag_ready, sc_ready, probs_ready = sem("qdiag_ready"), sem("sc_ready"), sem("probs_ready")
        num_ready, a_ready, a_hi_ready, a_lo_ready = sem("num_ready"), sem("a_ready"), sem("a_hi_ready"), sem("a_lo_ready")
        kt_ps, ktok_ready, state_ready, kv_ready = sem("kt_ps"), sem("ktok_ready"), sem("state_ready"), sem("kv_ready")
        op_ready, y_gated, xr_ready, y_ready = sem("op_ready"), sem("y_gated"), sem("xr_ready"), sem("y_ready")

        x_groups = x.rearrange("a (g t p) d -> (a g) p t d", t=GT, p=P)
        x_tiles = x.rearrange("a (t p) d -> (a t) p d", p=P)
        mid_tiles = x_mid.rearrange("(t p) d -> t p d", p=P)

        def unit_of(u):
            return (u % 2, u // 2) if u < 2 * C else (2, u - 2 * C)

        block = s.enter_context(nc.Block())

        @block.sync
        def _(sp):
            def load_group(g):
                wait(sp, xt_ps, C * g)
                sp.dma_start(xg[:, :, :], x_groups[g, :, :, :] if isinstance(g, int) else
                             x_groups[bass.ds(g, 1), :, :, :].rearrange("a p t d -> (a p) t d")).then_inc(x_in, 16)

            def load_residual(tile, slot):
                wait(sp, y_ready, tile - 1)
                sp.dma_start(x_res[:, slot, :], x_tiles[tile, :, :] if isinstance(tile, int) else
                             x_tiles[bass.ds(tile, 1), :, :].rearrange("a p d -> (a p) d")).then_inc(xr_in[slot], 16)

            def store(tile, slot):
                wait(sp, y_ready, tile + 1)
                sp.dma_start(mid_tiles[tile, :, :] if isinstance(tile, int) else
                             mid_tiles[bass.ds(tile, 1), :, :].rearrange("a p d -> (a p) d"),
                             y[:, slot, :]).then_inc(y_out[slot], 16)

            load_group(0)
            load_group(1)

            def group(g, parity):
                if not isinstance(g, int) or g + 2 < NG:
                    load_group(g + 2)
                for t in range(GT):
                    tile = g * GT + t
                    load_residual(tile, t % 2)
                    if not isinstance(tile, int) or tile > 0:
                        store(tile - 1, (t + 1) % 2)

            groups(sp, 2, NG - 2, group)
            store(NG * GT - 1, 1)
            for slot in range(2):
                sp.wait_ge(y_out[slot], 16 * NG * GT // 2)

        @block.gpsimd
        def _(pool):
            def rstd_of(g):
                wait(pool, var_ready, g + 1)
                pool.tensor_tensor(out=rstd[:, :], in0=var_eps[:, :], in1=half_neg[:, :], op=ALU.pow).then_inc(rstd_ready, 1)

            def exp_part(g, n):
                wait(pool, exp_ready, g * 2 * C + n + 1)
                if not isinstance(g, int):
                    pool.sem_inc(pool_passed, 1)
                pool.tensor_scalar(z_exp[:, n % 2, :], z_exp[:, n % 2, :], 1.0, EPS_FEAT, ALU.min,
                                   ALU.add).then_inc(emin_ready, 1)

            def q_times_sum(g, parity, c):
                wait(pool, ksum_ready, g * C + c + 1)
                wait(pool, phi_ready, g * 2 * C + 2 * c + 2)
                wait(pool, prod_lo_ready, g * C + c)
                pool.tensor_tensor(out=prod[:, :], in0=k_sum[:, c, :], in1=qt[parity][:, c, :],
                                   op=ALU.mult).then_inc(prod_ready, 1)

            def prod_low(g, c):
                wait(pool, prod_hi_ready, g * C + c + 1)
                pool.tensor_tensor(out=prod_lo[:, :], in0=prod[:, :], in1=prod_hi[:, :].bitcast(F32),
                                   op=ALU.subtract).then_inc(prod_lo_ready, 1)

            def a_low(tile):
                wait(pool, a_hi_ready, tile + 1)
                pool.tensor_tensor(out=a_lo[:, :], in0=a_t[:, :], in1=a_hi[:, :].bitcast(F32),
                                   op=ALU.subtract).then_inc(a_lo_ready, 1)

            def residual(tile, slot, uses):
                wait(pool, xr_in[slot], 16 * (uses + 1))
                pool.tensor_tensor(out=x_res[:, slot, :], in0=x_res[:, slot, :], in1=gabo_row[:, :],
                                   op=ALU.add).then_inc(xr_ready, 1)
                wait(pool, xr_ready, tile + 1)
                wait(pool, y_gated, tile + 1)
                pool.tensor_tensor(out=y[:, slot, :], in0=y[:, slot, :], in1=x_res[:, slot, :],
                                   op=ALU.add).then_inc(y_ready, 1)

            def last_residual(g, t):
                tile = g * GT + t - 1
                if not isinstance(tile, int) or tile >= 0:
                    residual(tile, (t + 1) % 2, g * 2 + (t - 1) // 2)

            rstd_of(0)
            for c in range(C):
                exp_part(0, 2 * c)
                exp_part(0, 2 * c + 1)
                q_times_sum(0, 0, c)
                prod_low(0, c)
            rstd_of(1)

            def group(g, parity):
                ahead = not isinstance(g, int) or g + 1 < NG
                two_ahead = not isinstance(g, int) or g + 2 < NG
                n = g + 1
                if ahead:
                    exp_part(n, 0)
                last_residual(g, 0)
                if ahead:
                    exp_part(n, 1)
                    q_times_sum(n, 1 - parity, 0)
                a_low(g * GT)
                if ahead:
                    exp_part(n, 2)
                    prod_low(n, 0)
                    exp_part(n, 3)
                    exp_part(n, 4)
                    q_times_sum(n, 1 - parity, 1)
                last_residual(g, 1)
                if ahead:
                    exp_part(n, 5)
                    prod_low(n, 1)
                a_low(g * GT + 1)
                if ahead:
                    exp_part(n, 6)
                    exp_part(n, 7)
                    q_times_sum(n, 1 - parity, 2)
                    prod_low(n, 2)
                if two_ahead:
                    rstd_of(g + 2)
                if ahead:
                    q_times_sum(n, 1 - parity, 3)
                last_residual(g, 2)
                if ahead:
                    prod_low(n, 3)
                a_low(g * GT + 2)
                last_residual(g, 3)
                a_low(g * GT + 3)

            groups(pool, 2, NG - 2, group)
            residual(NG * GT - 1, 1, NG * 2 - 1)

        @block.scalar
        def _(act):
            def xt_high(g, c):
                wait(act, xt_ps, g * C + c + 1)
                act.activation(xt_hi[:, c, :], den_tp[:, :], ACT.Copy, scale=scale_col[:, c:c + 1]).then_inc(xt_hi_done, 1)

            def exp_relu(g, n):
                kind, c = unit_of(n)
                bias = qk_bias[:, 1 - kind, c:c + 1]
                wait(act, pj_ready, g * UNITS + n + 1)
                wait(act, phi_ready, g * 2 * C + n - 1)
                act.activation(z_exp[:, n % 2, :], pj[:, n % 2, :], ACT.Exp, bias=bias).then_inc(exp_ready, 1)
                act.activation(z_relu[:, n % 2, :], pj[:, n % 2, :], ACT.Relu, bias=bias).then_inc(relu_ready, 1)

            def prod_high(g, c):
                wait(act, prod_ready, g * C + c + 1)
                wait(act, den_ps, g * C + c)
                act.activation(prod_hi[:, :], prod[:, :], ACT.Copy).then_inc(prod_hi_ready, 1)

            def den_out(g, parity, c):
                wait(act, den_ps, g * C + c + 1)
                act.activation(r_den[parity][:, c, :], den_tp[:, :], ACT.Copy, bias=EPS_DEN).then_inc(den_ready, 1)

            def q_blocks(tile, g, parity, t):
                wait(act, phi_ready, (g + 1) * 2 * C)
                wait(act, sc_ready, tile * C)
                for h in range(HPC):
                    rows = slice(h * E, (h + 1) * E)
                    ins = act.activation(q_diag[rows, :, h, :], qt[parity][rows, :, t * P:(t + 1) * P], ACT.Copy)
                ins.then_inc(qdiag_ready, 1)

            def k_rows(tile, t):
                wait(act, kt_ps, tile + 1)
                wait(act, state_ready, tile - 1)
                act.activation(k_tok[:, t % 2, :], kt_op[:, :], ACT.Copy).then_inc(ktok_ready, 1)

            def a_high(tile):
                wait(act, a_ready, tile + 1)
                wait(act, op_ready, tile)
                act.activation(a_hi[:, :], a_t[:, :], ACT.Copy).then_inc(a_hi_ready, 1)

            act.wait_ge(init_done, 1)
            for c in range(C):
                xt_high(0, c)
            for c in range(C):
                exp_relu(0, 2 * c)
                exp_relu(0, 2 * c + 1)
                prod_high(0, c)
                den_out(0, 0, c)
            for c in range(C):
                xt_high(1, c)
            q_blocks(0, 0, 0, 0)

            def group(g, parity):
                ahead = not isinstance(g, int) or g + 1 < NG
                two_ahead = not isinstance(g, int) or g + 2 < NG
                n = g + 1
                other = 1 - parity
                if ahead:
                    exp_relu(n, 0)
                    exp_relu(n, 1)
                k_rows(g * GT, 0)
                q_blocks(g * GT + 1, g, parity, 1)
                a_high(g * GT)
                if ahead:
                    exp_relu(n, 2)
                    prod_high(n, 0)
                    exp_relu(n, 3)
                    exp_relu(n, 4)
                    den_out(n, other, 0)
                    exp_relu(n, 5)
                    prod_high(n, 1)
                k_rows(g * GT + 1, 1)
                q_blocks(g * GT + 2, g, parity, 2)
                a_high(g * GT + 1)
                if ahead:
                    exp_relu(n, 6)
                    exp_relu(n, 7)
                    den_out(n, other, 1)
                    prod_high(n, 2)
                    den_out(n, other, 2)
                    prod_high(n, 3)
                k_rows(g * GT + 2, 2)
                q_blocks(g * GT + 3, g, parity, 3)
                a_high(g * GT + 2)
                if ahead:
                    den_out(n, other, 3)
                if two_ahead:
                    xt_high(g + 2, 0)
                    xt_high(g + 2, 1)
                k_rows(g * GT + 3, 3)
                if ahead:
                    q_blocks(g * GT + 4, n, other, 0)
                a_high(g * GT + 3)
                if two_ahead:
                    xt_high(g + 2, 2)
                    xt_high(g + 2, 3)

            groups(act, 2, NG - 2, group)

        @block.vector
        def _(dve):
            def norm_stats(g):
                wait(dve, x_in, 16 * (g + 1))
                for t in range(GT):
                    ins = dve.bn_stats(stats[:, t, :], xg[:, t, :])
                ins.then_inc(ln_chain, 1)

            def norm_var(g):
                wait(dve, ln_chain, 2 * g + 1)
                wait(dve, xn_ready, g)
                if not isinstance(g, int):
                    dve.sem_inc(dve_passed, 1)
                for t in range(GT):
                    ins = dve.bn_aggr(mean_var[:, t, :], stats[:, t, :])
                ins.then_inc(ln_chain, 1)
                wait(dve, ln_chain, 2 * g + 2)
                dve.tensor_scalar(var_eps[:, :], mean_var[:, :, 1], EPS_LN, None, ALU.add).then_inc(var_ready, 1)

            def norm_x(g):
                wait(dve, rstd_ready, g + 1)
                for t in range(GT):
                    ins = dve.tensor_scalar(xg[:, t, :], xg[:, t, :], mean_var[:, t, 0:1], rstd[:, t:t + 1],
                                            ALU.subtract, ALU.mult)
                ins.then_inc(xn_ready, 1)

            def xt_low(g, c):
                wait(dve, xt_hi_done, g * C + c + 1)
                dve.scalar_tensor_tensor(out=xt_lo[:, c, :], in0=den_tp[:, :], scalar=scale_col[:, c:c + 1],
                                         in1=xt_hi[:, c, :].bitcast(F32), op0=ALU.mult,
                                         op1=ALU.subtract).then_inc(xt_lo_done, 1)

            def feature(g, parity, n):
                kind, c = unit_of(n)
                to = (kt, qt)[kind][parity]
                wait(dve, emin_ready, g * 2 * C + n + 1)
                wait(dve, relu_ready, g * 2 * C + n + 1)
                dve.tensor_tensor(out=to[:, c, :], in0=z_exp[:, n % 2, :], in1=z_relu[:, n % 2, :],
                                  op=ALU.add).then_inc(phi_ready, 1)
                if kind == 0:
                    wait(dve, phi_ready, g * 2 * C + n + 1)
                    wait(dve, prod_ready, (g - 1) * C + c + 1)
                    first = isinstance(g, int) and g == 0
                    dve.tensor_tensor_scan(k_sum[:, c, :], to[:, c, :], to[:, c, :],
                                           0.0 if first else k_sum[:, c, GN - 1:GN],
                                           ALU.add, ALU.bypass).then_inc(ksum_ready, 1)

            def v_rows(g, parity, t):
                wait(dve, pj_ready, g * UNITS + 2 * C + t + 1)
                dve.tensor_tensor(out=v[parity][:, t, :], in0=pj[:, t % 2, :], in1=bv_row[:, :],
                                  op=ALU.add).then_inc(v_ready, 1)

            def recip(g, parity, c):
                wait(dve, den_ready, g * C + c + 1)
                dve.reciprocal(r_den[parity][:, c, :], r_den[parity][:, c, :]).then_inc(rden_ready, 1)

            def mask(tile, c):
                wait(dve, sc_ready, tile * C + c + 1)
                dve.tensor_tensor(out=probs[:, c, :].rearrange("p (h i) -> p h i", h=HPC),
                                  in0=sc[:, c % 2, :].rearrange("p (h i) -> p h i", h=HPC),
                                  in1=causal[:, :].rearrange("p (a i) -> p a i", a=1).broadcast_to([P, HPC, P]),
                                  op=ALU.mult).then_inc(probs_ready, 1)

            def divide(tile, g, parity, t):
                wait(dve, num_ready, tile + 1)
                wait(dve, rden_ready, (g + 1) * C)
                wait(dve, a_lo_ready, tile)
                dve.tensor_tensor(out=a_t[:, :].rearrange("p (c i) -> p c i", c=C),
                                  in0=num[:, :].rearrange("p (c i) -> p c i", c=C),
                                  in1=r_den[parity][:, :, t * P:(t + 1) * P], op=ALU.mult).then_inc(a_ready, 1)

            def state_out(tile):
                wait(dve, state_ready, tile + 1)
                dve.tensor_tensor(out=kv_diag[:, :, :], in0=state[:, :].rearrange("p (c f) -> p c f", c=C),
                                  in1=head_diag[:, :].rearrange("p (a f) -> p a f", a=1).broadcast_to([P, C, P]),
                                  op=ALU.mult).then_inc(kv_ready, 1)

            def gate_y(tile, slot, uses):
                wait(dve, op_ready, tile + 1)
                wait(dve, y_out[slot], 16 * uses)
                dve.tensor_tensor(out=y[:, slot, :], in0=kt_op[:, :], in1=ga_row[:, :],
                                  op=ALU.mult).then_inc(y_gated, 1)

            def gate_last(g, t):
                tile = g * GT + t - 1
                if not isinstance(tile, int) or tile >= 0:
                    gate_y(tile, (t + 1) % 2, g * 2 + (t - 1) // 2)

            dve.memset(q_diag[:, :, :, :], 0.0)
            dve.memset(kv_diag[:, :, :], 0.0)
            dve.memset(sc[:, :, :], 0.0).then_inc(init_done, 1)
            for g in range(2):
                norm_stats(g)
                norm_var(g)
                norm_x(g)
                if g == 0:
                    for c in range(C):
                        xt_low(0, c)
                    for n in range(2 * C):
                        feature(0, 0, n)
                    for t in range(GT):
                        v_rows(0, 0, t)
            recip(0, 0, 0)
            recip(0, 0, 1)
            for c in range(C):
                xt_low(1, c)

            def group(g, parity):
                ahead = not isinstance(g, int) or g + 1 < NG
                two_ahead = not isinstance(g, int) or g + 2 < NG
                n = g + 1
                other = 1 - parity
                for t in range(GT):
                    tile = g * GT + t
                    mask(tile, 0)
                    mask(tile, 1)
                    if t == 0:
                        recip(g, parity, 2)
                    elif t < 3 and ahead:
                        recip(n, other, t - 1)
                    if ahead and t < 2:
                        feature(n, other, 4 * t)
                    elif ahead and t == 2:
                        v_rows(n, other, 0)
                    elif two_ahead and t == 3:
                        xt_low(g + 2, 0)
                    gate_last(g, t)
                    mask(tile, 2)
                    mask(tile, 3)
                    if t == 0:
                        recip(g, parity, 3)
                    if ahead and t < 2:
                        feature(n, other, 4 * t + 1)
                    elif ahead and t == 2:
                        v_rows(n, other, 1)
                    elif two_ahead and t == 3:
                        xt_low(g + 2, 1)
                    if two_ahead and t == 1:
                        norm_stats(g + 2)
                    divide(tile, g, parity, t)
                    if ahead and t < 2:
                        feature(n, other, 4 * t + 2)
                    elif ahead and t == 2:
                        v_rows(n, other, 2)
                    elif two_ahead and t == 3:
                        xt_low(g + 2, 2)
                    state_out(tile)
                    if two_ahead and t == 1:
                        norm_var(g + 2)
                    if ahead and t < 2:
                        feature(n, other, 4 * t + 3)
                    elif ahead and t == 2:
                        v_rows(n, other, 3)
                    elif two_ahead and t == 3:
                        xt_low(g + 2, 3)
                    if two_ahead and t == 2:
                        norm_x(g + 2)

            groups(dve, 2, NG - 2, group)
            gate_y(NG * GT - 1, 1, NG * 2 - 1)

        @block.tensor
        def _(pe):
            def x_turn(g, c):
                wait(pe, xn_ready, g + 1)
                if c == 0:
                    wait(pe, den_ready, g * C)
                else:
                    wait(pe, xt_lo_done, g * C + c)
                for t in range(GT):
                    mm = pe.transpose(den_tp[:, t * P:(t + 1) * P], xg[:, t, c * P:(c + 1) * P], ident[:, :])
                mm.then_inc(xt_ps, 1)

            def project(g, u):
                kind, c = unit_of(u)
                if u == 0:
                    wait(pe, xt_lo_done, (g + 1) * C)
                if u < 2:
                    wait(pe, v_ready, (g - 1) * C + u + 3)
                elif u < 2 * C + 2:
                    wait(pe, relu_ready, g * 2 * C + u - 1)
                else:
                    wait(pe, v_ready, g * C + u - 2 * C - 1)
                to = pj[:, u % 2, :]
                passes = [(hi_w, hi_x, k) for hi_w, hi_x in ((1, 1), (1, 0), (0, 1)) for k in range(C)]
                for i, (hi_w, hi_x, k) in enumerate(passes):
                    w = w_hi if hi_w else w_lo
                    xt = xt_hi if hi_x else xt_lo
                    if kind == 2:
                        mm = pe.matmul(to, xt[:, k, c * P:(c + 1) * P], w[:, k, WV:WV + D],
                                       start=(i == 0), stop=(i == len(passes) - 1))
                    else:
                        at = (WK, WQ)[kind] + c * P
                        mm = pe.matmul(to, w[:, k, at:at + P], xt[:, k, :],
                                       start=(i == 0), stop=(i == len(passes) - 1))
                mm.then_inc(pj_ready, 1)

            def denominators(g, c):
                wait(pe, prod_lo_ready, g * C + c + 1)
                if c == 0:
                    wait(pe, xt_lo_done, (g + 1) * C)
                else:
                    wait(pe, den_ready, g * C + c)
                pe.matmul(den_tp[:, :], head_ones[:, :], prod_hi[:, :], start=True, stop=False)
                pe.matmul(den_tp[:, :], head_ones[:, :], prod_lo[:, :], start=False, stop=True).then_inc(den_ps, 1)

            def scores(tile, parity, t, c):
                if c == 0:
                    wait(pe, qdiag_ready, tile + 1)
                wait(pe, probs_ready, tile * C + c - 1)
                bank = sc[:, c % 2, :].rearrange("p (h i) -> p h i", h=HPC)
                for j in range(0, P, 32):
                    mm = pe.matmul(bank[j:j + 32, :, j:P], kt[parity][:, c, t * P + j:t * P + j + 32],
                                   q_diag[:, c, :, j:P], start=True, stop=True)
                mm.then_inc(sc_ready, 1)

            def k_turn(tile, parity, t):
                wait(pe, y_gated, tile)
                for c in range(C):
                    mm = pe.transpose(kt_op[:, c * P:(c + 1) * P], kt[parity][:, c, t * P:(t + 1) * P], ident[:, :])
                mm.then_inc(kt_ps, 1)

            def numerators(tile, g, parity, t):
                wait(pe, kv_ready, tile)
                wait(pe, a_ready, tile)
                for c in range(C):
                    pe.matmul(num[:, c * P:(c + 1) * P], kv_diag[:, c, :], qt[parity][:, c, t * P:(t + 1) * P],
                              start=(c == 0), stop=False, skip_group_check=True)
                wait(pe, v_ready, g * C + t + 1)
                for c in range(C):
                    wait(pe, probs_ready, tile * C + c + 1)
                    for h in range(HPC):
                        f = c * P + h * E
                        mm = pe.matmul(num[h * E:(h + 1) * E, c * P:(c + 1) * P], v[parity][:, t, f:f + E],
                                       probs[:, c, h * P:(h + 1) * P], start=False, stop=(c == C - 1),
                                       skip_group_check=True)
                mm.then_inc(num_ready, 1)

            def add_state(tile, parity, t):
                wait(pe, ktok_ready, tile + 1)
                for c in range(C):
                    f = slice(c * P, (c + 1) * P)
                    mm = pe.matmul(state[:, f], k_tok[:, t % 2, f], v[parity][:, t, f], start=False, stop=False,
                                   skip_group_check=True)
                mm.then_inc(state_ready, 1)

            def out_project(tile):
                wait(pe, a_lo_ready, tile + 1)
                wait(pe, ktok_ready, tile + 1)
                passes = [(a, w, c) for a, w in ((a_hi, w_hi), (a_hi, w_lo), (a_lo, w_hi)) for c in range(C)]
                for i, (a, w, c) in enumerate(passes):
                    mm = pe.matmul(kt_op[:, :], a[:, c * P:(c + 1) * P], w[:, c, WO:WO + D],
                                   start=(i == 0), stop=(i == len(passes) - 1))
                mm.then_inc(op_ready, 1)

            pe.wait_ge(init_done, 1)
            pe.matmul(state[:, :], kv_diag[:, 0, :], q_diag[:, 0, :, :].rearrange("p h i -> p (h i)"),
                      start=True, stop=False, skip_group_check=True)
            for c in range(C):
                x_turn(0, c)
            for u in range(UNITS):
                project(0, u)
                if u >= 3 and u % 2:
                    if (u - 3) // 2 < C:
                        denominators(0, (u - 3) // 2)
            for c in range(C):
                x_turn(1, c)

            def group(g, parity):
                ahead = not isinstance(g, int) or g + 1 < NG
                two_ahead = not isinstance(g, int) or g + 2 < NG
                n = g + 1
                for t in range(GT):
                    tile = g * GT + t

                    def fill(i):
                        if t < 3 and ahead:
                            project(n, 4 * t + i)
                        elif t == 3 and two_ahead:
                            x_turn(g + 2, i)

                    scores(tile, parity, t, 0)
                    scores(tile, parity, t, 1)
                    fill(0)
                    if not isinstance(tile, int) or tile > 0:
                        out_project(tile - 1)
                    scores(tile, parity, t, 2)
                    scores(tile, parity, t, 3)
                    fill(1)
                    if t == 2 and ahead:
                        denominators(n, 2)
                    k_turn(tile, parity, t)
                    numerators(tile, g, parity, t)
                    fill(2)
                    if t == 1 and ahead:
                        denominators(n, 1)
                    add_state(tile, parity, t)
                    fill(3)
                    if t in (0, 2) and ahead:
                        denominators(n, 0 if t == 0 else 3)

            groups(pe, 2, NG - 2, group)
            out_project(NG * GT - 1)


def load_ffn(nc, sem, sbuf, psum, ident, shift_col, wg, wu, wd, gu_bias, wide, w_gate_t, w_up_t, w_down_t):
    with ExitStack() as s:
        RING = 2
        raw = sbuf(s, "raw", [P, RING, HID], I32)
        word = sbuf(s, "word", [P, RING, HID])
        short = sbuf(s, "short", [P, RING, HID], F32R)
        rest = sbuf(s, "rest", [P, RING, HID])
        most = sbuf(s, "most", [P, 3 * C])
        any_most = sbuf(s, "any_most", [P, 1])
        ones = sbuf(s, "ones2", [P, P])
        sb_bc = sbuf(s, "sb_bc", [P, C, P])
        bias_row = sbuf(s, "bias_row", [P, 2, HID])
        banks = psum(s, "load_banks", [P, 8, 512])
        raw_in = [sem(f"raw_in{i}") for i in range(RING)]
        w_moved = [sem(f"w_moved{i}") for i in range(RING)]
        word_ready, short_ready, rest_ready, most_ready = (sem("word_ready"), sem("short_ready"), sem("rest_ready"),
                                                           sem("most_ready"))
        chain, sb_ready, bias_mm, bias_ev, bias_tp, bias_out = (sem("load_chain"), sem("sb_ready"), sem("bias_mm2"),
                                                                sem("bias_ev2"), sem("bias_tp"), sem("bias_out"))
        sum_ready, flag_done = sem("sum_ready"), sem("flag_done")

        pieces = [(w_gate_t[k * P:(k + 1) * P, :], wg[:, k, :]) for k in range(C)]
        pieces += [(w_up_t[k * P:(k + 1) * P, :], wu[:, k, :]) for k in range(C)]
        pieces += [(w_down_t[k * 3 * P:(k + 1) * 3 * P, :].rearrange("(h p) n -> p h n", p=P),
                    wd[:, 3 * k:3 * k + 3, :]) for k in range(C)]

        def as_piece(ap, to):
            return ap if len(to.shape) == 2 else ap.rearrange("p (h n) -> p h n", h=3)

        with nc.Block() as block:
            @block.sync
            def _(sp):
                for i, (src, to) in enumerate(pieces):
                    wait(sp, word_ready, i - RING + 1)
                    sp.dma_start(as_piece(raw[:, i % RING, :], to), src).then_inc(raw_in[i % RING], 16)

            @block.scalar
            def _(act):
                for i, (src, to) in enumerate(pieces):
                    act.wait_ge(raw_in[i % RING], 16 * (i // RING + 1))
                    wait(act, w_moved[i % RING], 16 * (i // RING))
                    wait(act, rest_ready, i - RING + 1)
                    act.activation(word[:, i % RING, :], raw[:, i % RING, :], ACT.Copy).then_inc(word_ready, 1)
                    act.wait_ge(word_ready, i + 1)
                    act.dma_start(to.bitcast(F32), as_piece(word[:, i % RING, :], to)).then_inc(w_moved[i % RING], 16)
                for r in range(RING):
                    act.wait_ge(w_moved[r], 16 * (len(pieces) // RING))

            @block.vector
            def _(dve):
                dve.memset(ones[:, :], 1.0).then_inc(chain, 1)
                dve.wait_ge(chain, 1)
                for k in range(C):
                    ins = dve.tensor_scalar(sb_bc[:, k, :], ones[:, :], shift_col[:, k:k + 1], None, ALU.mult)
                ins.then_inc(sb_ready, 1)
                for i in range(len(pieces)):
                    r = i % RING
                    dve.wait_ge(word_ready, i + 1)
                    dve.tensor_copy(short[:, r, :], word[:, r, :]).then_inc(short_ready, 1)
                    dve.wait_ge(short_ready, i + 1)
                    dve.tensor_tensor(out=rest[:, r, :], in0=word[:, r, :], in1=short[:, r, :].bitcast(F32),
                                      op=ALU.not_equal).then_inc(rest_ready, 1)
                    dve.wait_ge(rest_ready, i + 1)
                    dve.tensor_reduce(most[:, i:i + 1], rest[:, r, :], AX.X, ALU.max).then_inc(most_ready, 1)
                dve.wait_ge(most_ready, len(pieces))
                dve.tensor_reduce(any_most[:, :], most[:, :], AX.X, ALU.max).then_inc(most_ready, 1)
                for n in range(6):
                    dve.wait_ge(bias_mm, n + 1)
                    dve.tensor_copy(bias_row[:, n // 3, (n % 3) * 512:(n % 3 + 1) * 512],
                                    banks[:, n, :]).then_inc(bias_ev, 1)
                for m in range(2):
                    for b in range(3):
                        n = 3 * m + b
                        dve.wait_ge(bias_tp, n + 1)
                        scale = W_SCALE if m == 0 else 1.0
                        dve.tensor_scalar(gu_bias[:, m, 4 * b:4 * b + 4], banks[:, n, 0:512:P], scale, None,
                                          ALU.mult).then_inc(bias_out, 1)
                dve.wait_ge(sum_ready, 1)
                dve.tensor_scalar(wide[:, :], banks[0:1, 7, 0:1], 0.5, None, ALU.is_gt).then_inc(flag_done, 1)
                dve.wait_ge(flag_done, 1)

            @block.tensor
            def _(pe):
                pe.wait_ge(sb_ready, 1)
                for r in range(RING):
                    pe.wait_ge(w_moved[r], 16 * (2 * C // RING))
                for n in range(6):
                    w = (wg, wu)[n // 3]
                    for k in range(C):
                        mm = pe.matmul(banks[:, n, :], sb_bc[:, k, :],
                                       w[:, k, (n % 3) * 512:(n % 3 + 1) * 512].bitcast(F32),
                                       start=(k == 0), stop=(k == C - 1))
                    mm.then_inc(bias_mm, 1)
                pe.wait_ge(most_ready, len(pieces) + 1)
                pe.matmul(banks[0:1, 7, 0:1], any_most[:, :], ones[:, 0:1], start=True, stop=True).then_inc(sum_ready, 1)
                for n in range(6):
                    pe.wait_ge(bias_ev, n + 1)
                    for j in range(4):
                        at = (n % 3) * 512 + j * P
                        mm = pe.transpose(banks[:, n, j * P:(j + 1) * P], bias_row[:, n // 3, at:at + P], ident[:, :])
                    mm.then_inc(bias_tp, 1)


def feed_forward(nc, sem, sbuf, psum, ident, scale_col, half_neg, wg, wu, wd, gu_bias, wide, gb_row, x_mid, out):
    with ExitStack() as s:
        xg = [sbuf(s, f"fx{i}", [P, GT, D]) for i in range(2)]
        xn = sbuf(s, "fxn", [P, GT, D])
        stats = sbuf(s, "fstats", [P, GT, 6])
        mean_var = sbuf(s, "fmean_var", [P, GT, 2])
        var_eps = sbuf(s, "fvar_eps", [P, GT])
        rstd = sbuf(s, "frstd", [P, GT])
        xt_hi = [sbuf(s, f"fxt_hi{i}", [P, C, GN], F32R) for i in range(2)]
        xt_lo = [sbuf(s, f"fxt_lo{i}", [P, C, GN], F32R) for i in range(2)]
        gate = sbuf(s, "gate", [P, 2, GN])
        h = sbuf(s, "h", [P, 2, GN])
        h_hi = sbuf(s, "h_hi", [P, HB, GN], F32R)
        h_lo = sbuf(s, "h_lo", [P, HB, GN], F32R)
        y = sbuf(s, "fy", [P, 2, D])
        gu = psum(s, "gu", [P, 4, 512])
        tp = psum(s, "tp", [P, 2, 512])
        dn = psum(s, "dn", [P, 2, 512])

        x_in, y_out = [sem(f"fx_in{i}") for i in range(2)], [sem(f"fy_out{i}") for i in range(2)]
        ln_chain, var_ready, rstd_ready, xn_ready = (sem("fln_chain"), sem("fvar_ready"), sem("frstd_ready"),
                                                     sem("fxn_ready"))
        xt_ps, xt_hi_done, xt_lo_done = sem("fxt_ps"), sem("fxt_hi_done"), sem("fxt_lo_done")
        gate_ps, up_ps, gate_ready, h_ready, h_hi_ready, h_lo_ready = (
            sem("gate_ps"), sem("up_ps"), sem("gate_ready"), sem("h_ready"), sem("h_hi_ready"), sem("h_lo_ready"))
        dn_ps, y_gated, y_ready, dve_passed = sem("dn_ps"), sem("fy_gated"), sem("fy_ready"), sem("fdve_passed")

        mid_groups = x_mid.rearrange("(g t p) d -> g p t d", t=GT, p=P)
        out_tiles = out.rearrange("a (t p) d -> (a t) p d", p=P)

        block = s.enter_context(nc.Block())

        @block.sync
        def _(sp):
            def load(g, parity):
                wait(sp, y_ready, (g - 1) * GT)
                sp.dma_start(xg[parity][:, :, :], mid_groups[g, :, :, :] if isinstance(g, int) else
                             mid_groups[bass.ds(g, 1), :, :, :].rearrange("a p t d -> (a p) t d")).then_inc(x_in[parity], 16)

            load(0, 0)

            def group(g, parity):
                if not isinstance(g, int) or g + 1 < NG:
                    load(g + 1, 1 - parity)
                for t in range(GT):
                    tile = g * GT + t
                    wait(sp, y_ready, tile + 1)
                    sp.dma_start(out_tiles[tile, :, :] if isinstance(tile, int) else
                                 out_tiles[bass.ds(tile, 1), :, :].rearrange("a p d -> (a p) d"),
                                 y[:, t % 2, :]).then_inc(y_out[t % 2], 16)

            groups(sp, 2, NG - 2, group)
            for slot in range(2):
                sp.wait_ge(y_out[slot], 16 * NG * GT // 2)

        @block.gpsimd
        def _(pool):
            def rstd_of(g):
                wait(pool, var_ready, g + 1)
                pool.tensor_tensor(out=rstd[:, :], in0=var_eps[:, :], in1=half_neg[:, :], op=ALU.pow).then_inc(rstd_ready, 1)

            def h_low(g, j):
                wait(pool, h_hi_ready, g * HB + j + 1)
                pool.tensor_tensor(out=h_lo[:, j, :], in0=h[:, j % 2, :], in1=h_hi[:, j, :].bitcast(F32),
                                   op=ALU.subtract).then_inc(h_lo_ready, 1)

            rstd_of(0)

            def group(g, parity):
                for j in range(HB):
                    h_low(g, j)
                    if j == 1 and (not isinstance(g, int) or g + 1 < NG):
                        rstd_of(g + 1)
                for t in range(GT):
                    wait(pool, y_gated, g * GT + t + 1)
                    pool.tensor_tensor(out=y[:, t % 2, :], in0=y[:, t % 2, :], in1=xg[parity][:, t, :],
                                       op=ALU.add).then_inc(y_ready, 1)

            groups(pool, 2, NG - 2, group)

        @block.scalar
        def _(act):
            def xt_high(g, parity, c):
                wait(act, xt_ps, g * C + c + 1)
                act.activation(xt_hi[parity][:, c, :], tp[:, c % 2, :], ACT.Copy,
                               scale=scale_col[:, c:c + 1]).then_inc(xt_hi_done, 1)

            for c in range(C):
                xt_high(0, 0, c)

            def group(g, parity):
                for j in range(HB):
                    n = g * HB + j
                    wait(act, gate_ps, n + 1)
                    wait(act, h_ready, n - 1)
                    act.activation(gate[:, j % 2, :], gu[:, 2 * (j % 2), :], ACT.Silu, bias=gu_bias[:, 0, j:j + 1],
                                   scale=W_SCALE).then_inc(gate_ready, 1)
                    wait(act, h_ready, n + 1)
                    act.activation(h_hi[:, j, :], h[:, j % 2, :], ACT.Copy).then_inc(h_hi_ready, 1)
                    if j >= 4 and j < 8 and (not isinstance(g, int) or g + 1 < NG):
                        xt_high(g + 1, 1 - parity, j - 4)

            groups(act, 2, NG - 2, group)

        @block.vector
        def _(dve):
            def norm_stats(g, parity):
                wait(dve, x_in[parity], 16 * (g // 2 + 1) if isinstance(g, int) else g * 8 + (16 - 8 * parity))
                wait(dve, ln_chain, 2 * g)
                for t in range(GT):
                    ins = dve.bn_stats(stats[:, t, :], xg[parity][:, t, :])
                ins.then_inc(ln_chain, 1)
                wait(dve, ln_chain, 2 * g + 1)
                wait(dve, xn_ready, g)
                if not isinstance(g, int):
                    dve.sem_inc(dve_passed, 1)
                for t in range(GT):
                    ins = dve.bn_aggr(mean_var[:, t, :], stats[:, t, :])
                ins.then_inc(ln_chain, 1)
                wait(dve, ln_chain, 2 * g + 2)
                dve.tensor_scalar(var_eps[:, :], mean_var[:, :, 1], EPS_LN, None, ALU.add).then_inc(var_ready, 1)

            def norm_x(g, parity):
                wait(dve, rstd_ready, g + 1)
                wait(dve, xt_ps, g * C)
                for t in range(GT):
                    ins = dve.tensor_scalar(xn[:, t, :], xg[parity][:, t, :], mean_var[:, t, 0:1], rstd[:, t:t + 1],
                                            ALU.subtract, ALU.mult)
                ins.then_inc(xn_ready, 1)

            def xt_low(g, parity, c):
                wait(dve, xt_hi_done, g * C + c + 1)
                dve.scalar_tensor_tensor(out=xt_lo[parity][:, c, :], in0=tp[:, c % 2, :], scalar=scale_col[:, c:c + 1],
                                         in1=xt_hi[parity][:, c, :].bitcast(F32), op0=ALU.mult,
                                         op1=ALU.subtract).then_inc(xt_lo_done, 1)

            norm_stats(0, 0)
            norm_x(0, 0)
            for c in range(C):
                xt_low(0, 0, c)

            def group(g, parity):
                ahead = not isinstance(g, int) or g + 1 < NG
                for j in range(HB):
                    n = g * HB + j
                    wait(dve, up_ps, n + 1)
                    wait(dve, gate_ready, n + 1)
                    wait(dve, h_lo_ready, n - 1)
                    dve.scalar_tensor_tensor(out=h[:, j % 2, :], in0=gu[:, 2 * (j % 2) + 1, :],
                                             scalar=gu_bias[:, 1, j:j + 1], in1=gate[:, j % 2, :], op0=ALU.add,
                                             op1=ALU.mult).then_inc(h_ready, 1)
                    if ahead and j == 0:
                        norm_stats(g + 1, 1 - parity)
                    if ahead and j == 2:
                        norm_x(g + 1, 1 - parity)
                    if ahead and 4 <= j < 8:
                        xt_low(g + 1, 1 - parity, j - 4)
                for t in range(GT):
                    wait(dve, dn_ps, g * GT + t + 1)
                    wait(dve, y_out[t % 2], g * 32 + 16 * (t // 2))
                    dve.tensor_tensor(out=y[:, t % 2, :], in0=dn[:, t % 2, :], in1=gb_row[:, :],
                                      op=ALU.mult).then_inc(y_gated, 1)

            groups(dve, 2, NG - 2, group)

        @block.tensor
        def _(pe):
            def x_turn(g, c):
                wait(pe, xn_ready, g + 1)
                wait(pe, xt_lo_done, g * C + c - 1)
                for t in range(GT):
                    mm = pe.transpose(tp[:, c % 2, t * P:(t + 1) * P], xn[:, t, c * P:(c + 1) * P], ident[:, :])
                mm.then_inc(xt_ps, 1)

            def passes(exact):
                return (lambda ap: ap) if exact else (lambda ap: ap.bitcast(F32))

            def all_groups(exact):
                as_ = passes(exact)

                def hidden(g, parity, j, w, bank, done):
                    for i, (xt, k) in enumerate((xt, k) for xt in (xt_hi, xt_lo) for k in range(C)):
                        mm = pe.matmul(gu[:, bank, :], as_(w[:, k, j * P:(j + 1) * P]), as_(xt[parity][:, k, :]),
                                       start=(i == 0), stop=(i == 2 * C - 1))
                    mm.then_inc(done, 1)

                def down(g, t):
                    wait(pe, y_gated, g * GT + t - 1)
                    for j in range(HB):
                        if t == 0:
                            wait(pe, h_lo_ready, g * HB + j + 1)
                        for half in (h_hi, h_lo):
                            mm = pe.matmul(dn[:, t % 2, :], as_(half[:, j, t * P:(t + 1) * P]), as_(wd[:, j, :]),
                                           start=(j == 0 and half is h_hi), stop=(j == HB - 1 and half is h_lo))
                    mm.then_inc(dn_ps, 1)

                def group(g, parity):
                    wait(pe, xt_lo_done, (g + 1) * C)
                    for j in range(HB):
                        n = g * HB + j
                        wait(pe, gate_ready, n - 1)
                        hidden(g, parity, j, wg, 2 * (j % 2), gate_ps)
                        wait(pe, h_ready, n - 1)
                        hidden(g, parity, j, wu, 2 * (j % 2) + 1, up_ps)
                        if 4 <= j < 8 and (not isinstance(g, int) or g + 1 < NG):
                            x_turn(g + 1, j - 4)
                    for t in range(GT):
                        down(g, t)

                groups(pe, 2, NG - 2, group)

            for c in range(C):
                x_turn(0, c)
            flag = pe.value_load(wide[0:1, 0:1])
            with pe.If(flag > 0):
                all_groups(False)
            with pe.Else():
                all_groups(True)


_INS = ["L0_attn_x", "L0_attn_W_qkv", "L0_attn_b_qkv", "L0_attn_W_out", "L0_attn_b_out",
        "L0_ffn_w_gate", "L0_ffn_w_up", "L0_ffn_w_down", "L0_c", "L0_wmod"]
_TURNED = ("L0_ffn_w_gate", "L0_ffn_w_up", "L0_ffn_w_down", "L0_c")


def kernel(**inputs):
    import concourse.bacc as bacc
    from concourse.bass_utils import run_bass_kernel_spmd

    nc = bacc.Bacc("TRN2", target_bir_lowering=False, num_devices=1, dynamic_dma_scratch_size=1024)
    arrays, args = {}, []
    for name in _INS:
        a = np.asarray(inputs[name])
        if name == "L0_c":
            a = a.reshape(C, P)
        a = np.ascontiguousarray(a.T if name in _TURNED else a)
        arrays[f"in_{name}"] = a
        args.append(nc.dram_tensor(f"in_{name}", a.shape, mybir.dt.from_np(a.dtype), kind="ExternalInput").ap())
    out = nc.dram_tensor("out", (1, L, D), F32, kind="ExternalOutput").ap()
    build(nc, *args, out)
    r = run_bass_kernel_spmd(nc, [arrays], core_ids=[0])
    return r.results[0]["out"]
```

```python
from contextlib import ExitStack

import numpy as np

import concourse.bass as bass
from concourse import mybir

F32 = mybir.dt.float32
F32R = mybir.dt.float32r
I32 = mybir.dt.int32
ALU = mybir.AluOpType
ACT = mybir.ActivationFunctionType
AX = mybir.AxisListType

P = 128
L = 8192
D = 512
HID = 1536
E = 32
C = D // P
HB = HID // P
HPC = P // E
GT = 4
GN = GT * P
NG = L // GN
UNITS = 3 * C
EPS_LN = 1e-5
EPS_FEAT = 1e-4
EPS_DEN = 1e-6
Q_SCALE = float(E) ** -0.5
EXACT = 4096.0
SA, CA, SB, CB = range(4)
W_SCALE = float(np.float32(1.0 / 127.0))


def wait(eng, sem, value):
    if not isinstance(value, int) or value > 0:
        eng.wait_ge(sem, value)


def groups(eng, first, last, body):
    for g in range(first):
        body(g, g % 2)
    with eng.Fori(first // 2, last // 2) as pair:
        for parity in range(2):
            body(pair * 2 + parity, parity)
    for g in range(last, NG):
        body(g, g % 2)


def build(nc, x, w_qkv, b_qkv, b_cols, w_out, b_out, w_gate_t, w_up_t, w_down_t, c_vec, w_mod, out):
    top = ExitStack()
    with top:
        def sem(name):
            return top.enter_context(nc.semaphore(name))

        def sbuf(stack, name, shape, dt=F32):
            return stack.enter_context(nc.sbuf_tensor(name, shape, dt))

        def psum(stack, name, shape):
            return stack.enter_context(nc.psum_tensor(name, shape, F32))

        x_mid = nc.dram_tensor("x_mid", (L, D), F32, kind="Internal").ap()

        ident = sbuf(top, "ident", [P, P])
        gb_row = sbuf(top, "gb_row", [P, D])
        mod_col = sbuf(top, "mod_col", [P, 4, C])
        half_neg = sbuf(top, "half_neg", [P, GT])
        wide = sbuf(top, "wide", [1, 1], I32)
        w_hi = sbuf(top, "w_hi", [P, C, 4 * D], F32R)
        w_lo = sbuf(top, "w_lo", [P, C, 4 * D], F32R)
        xt_hi = sbuf(top, "xt_hi", [P, C, GN], F32R)
        xt_lo = sbuf(top, "xt_lo", [P, C, GN], F32R)

        with ExitStack() as attn:
            ga_row = sbuf(attn, "ga_row", [P, D])
            gabo_row = sbuf(attn, "gabo_row", [P, D])
            bv_row = sbuf(attn, "bv_row", [P, D])
            qk_bias = sbuf(attn, "qk_bias", [P, 2, C])
            causal = sbuf(attn, "causal", [P, P])
            head_diag = sbuf(attn, "head_diag", [P, P])
            head_ones = sbuf(attn, "head_ones", [P, P], F32R)
            setup(nc, sem, sbuf, psum, ident, gb_row, mod_col, half_neg, w_hi, w_lo, ga_row, gabo_row,
                  bv_row, qk_bias, causal, head_diag, head_ones, w_qkv, b_qkv, b_cols, w_out, b_out, c_vec, w_mod)
            attention(nc, sem, sbuf, psum, ident, mod_col, half_neg, w_hi, w_lo, xt_hi, xt_lo, ga_row, gabo_row,
                      bv_row, qk_bias, causal, head_diag, head_ones, wide, x, w_gate_t, w_up_t, w_down_t, x_mid)
        feed_forward(nc, sem, sbuf, psum, ident, mod_col, half_neg, w_hi, w_lo, xt_hi, xt_lo, wide, gb_row,
                     w_gate_t, w_up_t, w_down_t, x_mid, out)


def setup(nc, sem, sbuf, psum, ident, gb_row, mod_col, half_neg, w_hi, w_lo, ga_row, gabo_row,
          bv_row, qk_bias, causal, head_diag, head_ones, w_qkv, b_qkv, b_cols, w_out, b_out, c_vec, w_mod):
    SAm, CAm, GAm, SBm, CBm, GBm = range(6)
    with ExitStack() as s:
        w_raw = sbuf(s, "w_raw", [P, C, 4 * D])
        wm = sbuf(s, "wm", [P, 2, C, D])
        bo_row = sbuf(s, "bo_row", [P, D])
        c_col = sbuf(s, "c_col", [P, C])
        c_exp = sbuf(s, "c_exp", [P, C])
        c_bc = sbuf(s, "c_bc", [P, C, P])
        ones = sbuf(s, "ones", [P, P])
        sign = sbuf(s, "sign", [P, D])
        size = sbuf(s, "size", [P, D])
        gate_row = sbuf(s, "gate_row", [P, D])
        banks = psum(s, "setup_banks", [P, 6, 512])

        c_in, b_in = sem("c_in"), sem("b_in")
        w_in = [sem(f"w_in{k}") for k in range(C)]
        wm_in = [sem(f"wm_in{m}") for m in range(6)]
        const_done, pool_chain, c_neg_exp = sem("const_done"), sem("pool_chain"), sem("c_neg_exp")
        dve_chain, c_ready, mod_mm, hi_done = sem("setup_dve_chain"), sem("c_ready"), sem("mod_mm"), sem("hi_done")
        order = (SAm, CAm, GAm, SBm, CBm, GBm)

        with nc.Block() as block:
            @block.sync
            def _(sp):
                sp.dma_start(c_col[:, :], c_vec).then_inc(c_in, 16)
                for i, m in enumerate(order):
                    wait(sp, mod_mm, i - 1)
                    sp.dma_start(wm[:, i % 2, :, :],
                                 w_mod[:, m * D:(m + 1) * D].rearrange("(c p) n -> p c n", p=P)).then_inc(wm_in[m], 16)

            @block.gpsimd
            def _(pool):
                pool.memset(ident[:, :], 0.0).then_inc(pool_chain, 1)
                pool.memset(causal[:, :], 1.0).then_inc(pool_chain, 1)
                pool.wait_ge(pool_chain, 2)
                pool.affine_select(out=ident[:, :], in_=ident[:, :], compare_op=ALU.not_equal, fill=1.0,
                                   base=0, pattern=[[-1, P]], channel_multiplier=1).then_inc(const_done, 1)
                pool.affine_select(out=causal[:, :], in_=causal[:, :], compare_op=ALU.is_ge, fill=0.0,
                                   base=0, pattern=[[1, P]], channel_multiplier=-1).then_inc(const_done, 1)

            @block.scalar
            def _(act):
                for k in range(C):
                    rows = slice(k * P, (k + 1) * P)
                    act.dma_start(w_raw[:, k, 0:3 * D], w_qkv[rows, :]).then_inc(w_in[k], 16)
                    act.dma_start(w_raw[:, k, 3 * D:4 * D], w_out[rows, :]).then_inc(w_in[k], 16)
                act.dma_start(qk_bias[:, :, :].rearrange("p a c -> p (a c)"), b_cols[:, 0:2 * C]).then_inc(b_in, 16)
                act.dma_start(bv_row[:, :], b_qkv[2 * D:3 * D].rearrange("(a n) -> a n", a=1).broadcast_to([P, D])).then_inc(b_in, 16)
                act.dma_start(bo_row[:, :], b_out.rearrange("(a n) -> a n", a=1).broadcast_to([P, D])).then_inc(b_in, 16)
                act.wait_ge(c_in, 16)
                act.activation(c_exp[:, :], c_col[:, :], ACT.Exp, scale=-1.0).then_inc(c_neg_exp, 1)
                for k in range(C):
                    act.wait_ge(w_in[k], 32)
                    act.activation(w_hi[:, k, :], w_raw[:, k, :], ACT.Copy).then_inc(hi_done, 1)

            @block.vector
            def _(dve):
                chain = [0]

                def link(ins):
                    chain[0] += 1
                    ins.then_inc(dve_chain, 1)
                    dve.wait_ge(dve_chain, chain[0])

                dve.memset(ones[:, :], 1.0)
                dve.memset(half_neg[:, :], -0.5)
                link(dve.memset(head_diag[:, :], 0.0))
                for h in range(HPC):
                    ins = dve.memset(head_diag[h * E:(h + 1) * E, h * E:(h + 1) * E], 1.0)
                link(ins)
                dve.tensor_copy(head_ones[:, :], head_diag[:, :])
                dve.wait_ge(c_neg_exp, 1)
                link(dve.tensor_scalar(c_exp[:, :], c_exp[:, :], 1.0, None, ALU.add))
                link(dve.reciprocal(c_exp[:, :], c_exp[:, :]))
                link(dve.tensor_tensor(out=c_col[:, :], in0=c_col[:, :], in1=c_exp[:, :], op=ALU.mult))
                for k in range(C):
                    ins = dve.tensor_scalar(c_bc[:, k, :], ones[:, :], c_col[:, k:k + 1], None, ALU.mult)
                ins.then_inc(c_ready, 1)
                dve.wait_ge(b_in, 48)
                dve.tensor_scalar(qk_bias[:, 0, :], qk_bias[:, 0, :], Q_SCALE, None, ALU.mult)

                def low_half(k):
                    dve.wait_ge(hi_done, k + 1)
                    dve.tensor_tensor(out=w_lo[:, k, :], in0=w_raw[:, k, :], in1=w_hi[:, k, :].bitcast(F32),
                                      op=ALU.subtract)

                for i, m in enumerate(order):
                    dve.wait_ge(mod_mm, i + 1)
                    if m in (GAm, GBm):
                        row = ga_row if m == GAm else gb_row
                        g = gate_row[:, :]
                        link(dve.tensor_copy(g, banks[:, i, :]))
                        link(dve.tensor_scalar(sign[:, :], g, 0.0, 2.0, ALU.is_ge, ALU.mult))
                        link(dve.tensor_scalar(sign[:, :], sign[:, :], -1.0, None, ALU.add))
                        link(dve.tensor_scalar(size[:, :], g, -1.0, 0.25, ALU.mult, ALU.max))
                        link(dve.tensor_tensor(out=size[:, :], in0=size[:, :], in1=g, op=ALU.max))
                        link(dve.tensor_tensor(out=row[:, :], in0=sign[:, :], in1=size[:, :], op=ALU.mult))
                    elif m in (CAm, CBm):
                        dve.tensor_scalar(mod_col[:, CA if m == CAm else CB, :], banks[:, i, 0:C], 1.0, None, ALU.add)
                    else:
                        dve.tensor_copy(mod_col[:, SA if m == SAm else SB, :], banks[:, i, 0:C])
                    if 0 < i <= C:
                        low_half(i - 1)
                dve.tensor_tensor(out=gabo_row[:, :], in0=ga_row[:, :], in1=bo_row[:, :], op=ALU.mult)
                link(dve.tensor_scalar(gb_row[:, :], gb_row[:, :], W_SCALE, W_SCALE, ALU.mult, ALU.mult))

            @block.tensor
            def _(pe):
                pe.wait_ge(c_ready, 1)
                for i, m in enumerate(order):
                    pe.wait_ge(wm_in[m], 16)
                    if m in (GAm, GBm):
                        for k in range(C):
                            mm = pe.matmul(banks[:, i, :], c_bc[:, k, :], wm[:, i % 2, k, :],
                                           start=(k == 0), stop=(k == C - 1))
                    else:
                        for c in range(C):
                            for k in range(C):
                                mm = pe.matmul(banks[:, i, c:c + 1], wm[:, i % 2, k, c * P:(c + 1) * P],
                                               c_col[:, k:k + 1], start=(k == 0), stop=(k == C - 1))
                    mm.then_inc(mod_mm, 1)


def ffn_pieces(w_gate_t, w_up_t, w_down_t):
    pieces = [w[k * P:(k + 1) * P, :] for w in (w_gate_t, w_up_t) for k in range(C)]
    return pieces + [w_down_t[k * 3 * P:(k + 1) * 3 * P, :].rearrange("(h p) n -> p h n", p=P) for k in range(C)]


def attention(nc, sem, sbuf, psum, ident, mod_col, half_neg, w_hi, w_lo, xt_hi, xt_lo, ga_row, gabo_row,
              bv_row, qk_bias, causal, head_diag, head_ones, wide, x, w_gate_t, w_up_t, w_down_t, x_mid):
    WQ, WK, WV, WO = 0, D, 2 * D, 3 * D
    with ExitStack() as s:
        xg = sbuf(s, "xg", [P, GT, D])
        stats = sbuf(s, "stats", [P, GT, 6])
        mean_var = sbuf(s, "mean_var", [P, GT, 2])
        var_eps = sbuf(s, "var_eps", [P, GT])
        rstd = sbuf(s, "rstd", [P, GT])
        z_exp = sbuf(s, "z_exp", [P, 2, GN])
        z_relu = sbuf(s, "z_relu", [P, 2, GN])
        xf = z_relu
        qt = [sbuf(s, f"qt{i}", [P, C, GN]) for i in range(2)]
        kt = [sbuf(s, f"kt{i}", [P, C, GN]) for i in range(2)]
        v = [sbuf(s, f"v{i}", [P, GT, D]) for i in range(2)]
        k_sum = sbuf(s, "k_sum", [P, C, GN])
        prod = sbuf(s, "prod", [P, GN])
        prod_hi = sbuf(s, "prod_hi", [P, GN], F32R)
        prod_lo = sbuf(s, "prod_lo", [P, GN], F32R)
        r_den = [sbuf(s, f"r_den{i}", [P, C, GN]) for i in range(2)]
        q_diag = sbuf(s, "q_diag", [P, C, HPC, P])
        probs = sbuf(s, "probs", [P, C, HPC * P])
        kv_diag = sbuf(s, "kv_diag", [P, C, P])
        k_tok = sbuf(s, "k_tok", [P, 2, D])
        a_t = sbuf(s, "a_t", [P, D])
        a_hi = sbuf(s, "a_hi", [P, D], F32R)
        a_lo = sbuf(s, "a_lo", [P, D], F32R)
        x_res = sbuf(s, "x_res", [P, 2, D])
        y = sbuf(s, "y", [P, 2, D])
        ones = sbuf(s, "ones_col", [P, 1])
        most = sbuf(s, "most", [P, 3 * C])
        beyond = sbuf(s, "beyond", [P, 1])
        pj = psum(s, "pj", [P, 2, 512])
        sc = psum(s, "sc", [P, 2, 512])
        num = psum(s, "num", [P, 512])
        state = psum(s, "state", [P, 512])
        den_tp = psum(s, "den_tp", [P, 512])
        kt_op = psum(s, "kt_op", [P, 512])
        turn_bank = [pj[:, 0, :], den_tp[:, :], pj[:, 1, :], den_tp[:, :]]

        init_done, pool_passed, dve_passed = sem("init_done"), sem("pool_passed"), sem("dve_passed")
        x_in, xr_in, y_out = sem("x_in"), [sem(f"xr_in{i}") for i in range(2)], [sem(f"y_out{i}") for i in range(2)]
        ln_chain, var_ready, rstd_ready, xn_ready = sem("ln_chain"), sem("var_ready"), sem("rstd_ready"), sem("xn_ready")
        xt_ps, xf_ready, xt_hi_done, xt_lo_done = sem("xt_ps"), sem("xf_ready"), sem("xt_hi_done"), sem("xt_lo_done")
        raw_in = [sem(f"raw_in{i}") for i in range(6)]
        ffn_w_ready, most_ready, beyond_ready, beyond_ps, wide_ready = (
            sem("ffn_w_ready"), sem("most_ready"), sem("beyond_ready"), sem("beyond_ps"), sem("wide_ready"))
        pj_ready, exp_ready, relu_ready, emin_ready, phi_ready = (sem("pj_ready"), sem("exp_ready"), sem("relu_ready"),
                                                                  sem("emin_ready"), sem("phi_ready"))
        v_ready, ksum_ready, prod_ready, prod_hi_ready, prod_lo_ready = (
            sem("v_ready"), sem("ksum_ready"), sem("prod_ready"), sem("prod_hi_ready"), sem("prod_lo_ready"))
        den_ps, den_ready, rden_ready = sem("den_ps"), sem("den_ready"), sem("rden_ready")
        qdiag_ready, sc_ready, probs_ready = sem("qdiag_ready"), sem("sc_ready"), sem("probs_ready")
        num_ready, a_ready, a_hi_ready, a_lo_ready = sem("num_ready"), sem("a_ready"), sem("a_hi_ready"), sem("a_lo_ready")
        kt_ps, ktok_ready, state_ready, kv_ready = sem("kt_ps"), sem("ktok_ready"), sem("state_ready"), sem("kv_ready")
        op_ready, y_gated, xr_ready, y_ready = sem("op_ready"), sem("y_gated"), sem("xr_ready"), sem("y_ready")

        x_groups = x.rearrange("a (g t p) d -> (a g) p t d", t=GT, p=P)
        x_tiles = x.rearrange("a (t p) d -> (a t) p d", p=P)
        mid_tiles = x_mid.rearrange("(t p) d -> t p d", p=P)
        mid_groups = x_mid.rearrange("(g t p) d -> g p t d", t=GT, p=P)
        raw = [buf[:, :, :].rearrange("p c n -> p (c n)")[:, 0:HID].bitcast(I32)
               for buf in (k_sum, xg, qt[0], kt[0], v[0], r_den[0])]
        RAW = len(raw)
        pieces = ffn_pieces(w_gate_t, w_up_t, w_down_t)

        def unit_of(u):
            return (u % 2, u // 2) if u < 2 * C else (2, u - 2 * C)

        block = s.enter_context(nc.Block())

        @block.sync
        def _(sp):
            def load_group(g):
                wait(sp, xt_ps, C * g)
                sp.dma_start(xg[:, :, :], x_groups[g, :, :, :] if isinstance(g, int) else
                             x_groups[bass.ds(g, 1), :, :, :].rearrange("a p t d -> (a p) t d")).then_inc(x_in, 16)

            def load_residual(tile, slot):
                wait(sp, y_ready, tile - 1)
                sp.dma_start(x_res[:, slot, :], x_tiles[tile, :, :] if isinstance(tile, int) else
                             x_tiles[bass.ds(tile, 1), :, :].rearrange("a p d -> (a p) d")).then_inc(xr_in[slot], 16)

            def store(tile, slot):
                wait(sp, y_ready, tile + 1)
                sp.dma_start(mid_tiles[tile, :, :] if isinstance(tile, int) else
                             mid_tiles[bass.ds(tile, 1), :, :].rearrange("a p d -> (a p) d"),
                             y[:, slot, :]).then_inc(y_out[slot], 16)

            def load_piece(i):
                if i == 0:
                    sp.wait_ge(prod_ready, NG * C)
                elif i == 1:
                    sp.wait_ge(xt_ps, (NG + 1) * C)
                elif i == 2:
                    sp.wait_ge(state_ready, (NG - 1) * GT)
                    sp.wait_ge(a_ready, (NG - 1) * GT)
                wait(sp, most_ready, i - RAW + 1)
                if i - RAW < 2 * C:
                    wait(sp, ffn_w_ready, i - RAW + 1)
                src = pieces[i]
                to = raw[i % RAW] if i < 2 * C else raw[i % RAW].rearrange("p (h n) -> p h n", h=3)
                sp.dma_start(to, src).then_inc(raw_in[i % RAW], 16)

            load_group(0)
            load_group(1)

            def group(g, parity):
                if not isinstance(g, int) or g + 2 < NG:
                    load_group(g + 2)
                elif g + 2 == NG:
                    sp.wait_ge(y_out[0], 16 * GT // 2)
                    sp.wait_ge(y_out[1], 16 * GT // 2)
                    sp.wait_ge(xt_ps, C * NG)
                    sp.dma_start(xg[:, :, :], mid_groups[0, :, :, :]).then_inc(x_in, 16)
                last = isinstance(g, int) and g == NG - 1
                if last:
                    for i in range(RAW):
                        load_piece(i)
                for t in range(GT):
                    tile = g * GT + t
                    load_residual(tile, t % 2)
                    if not isinstance(tile, int) or tile > 0:
                        store(tile - 1, (t + 1) % 2)
                    if last:
                        for i in ((), (6, 7), (8, 9, 10), (11,))[t]:
                            load_piece(i)

            groups(sp, 2, NG - 2, group)
            store(NG * GT - 1, 1)
            for slot in range(2):
                sp.wait_ge(y_out[slot], 16 * NG * GT // 2)

        @block.gpsimd
        def _(pool):
            def rstd_of(g):
                wait(pool, var_ready, g + 1)
                pool.tensor_tensor(out=rstd[:, :], in0=var_eps[:, :], in1=half_neg[:, :], op=ALU.pow).then_inc(rstd_ready, 1)

            def exp_part(g, n):
                wait(pool, exp_ready, g * 2 * C + n + 1)
                if not isinstance(g, int):
                    pool.sem_inc(pool_passed, 1)
                pool.tensor_scalar(z_exp[:, n % 2, :], z_exp[:, n % 2, :], 1.0, EPS_FEAT, ALU.min,
                                   ALU.add).then_inc(emin_ready, 1)

            def q_times_sum(g, parity, c):
                wait(pool, ksum_ready, g * C + c + 1)
                wait(pool, phi_ready, g * 2 * C + 2 * c + 2)
                wait(pool, prod_lo_ready, g * C + c)
                pool.tensor_tensor(out=prod[:, :], in0=k_sum[:, c, :], in1=qt[parity][:, c, :],
                                   op=ALU.mult).then_inc(prod_ready, 1)

            def prod_low(g, c):
                wait(pool, prod_hi_ready, g * C + c + 1)
                pool.tensor_tensor(out=prod_lo[:, :], in0=prod[:, :], in1=prod_hi[:, :].bitcast(F32),
                                   op=ALU.subtract).then_inc(prod_lo_ready, 1)

            def a_low(tile):
                wait(pool, a_hi_ready, tile + 1)
                pool.tensor_tensor(out=a_lo[:, :], in0=a_t[:, :], in1=a_hi[:, :].bitcast(F32),
                                   op=ALU.subtract).then_inc(a_lo_ready, 1)

            def residual(tile, slot, uses):
                wait(pool, xr_in[slot], 16 * (uses + 1))
                pool.tensor_tensor(out=x_res[:, slot, :], in0=x_res[:, slot, :], in1=gabo_row[:, :],
                                   op=ALU.add).then_inc(xr_ready, 1)
                wait(pool, xr_ready, tile + 1)
                wait(pool, y_gated, tile + 1)
                pool.tensor_tensor(out=y[:, slot, :], in0=y[:, slot, :], in1=x_res[:, slot, :],
                                   op=ALU.add).then_inc(y_ready, 1)

            def last_residual(g, t):
                tile = g * GT + t - 1
                if not isinstance(tile, int) or tile >= 0:
                    residual(tile, (t + 1) % 2, g * 2 + (t - 1) // 2)

            rstd_of(0)
            for c in range(C):
                exp_part(0, 2 * c)
                exp_part(0, 2 * c + 1)
                q_times_sum(0, 0, c)
                prod_low(0, c)
            rstd_of(1)

            def group(g, parity):
                ahead = not isinstance(g, int) or g + 1 < NG
                two_ahead = not isinstance(g, int) or g + 2 <= NG
                n = g + 1
                if ahead:
                    exp_part(n, 0)
                last_residual(g, 0)
                if ahead:
                    exp_part(n, 1)
                    q_times_sum(n, 1 - parity, 0)
                a_low(g * GT)
                if ahead:
                    exp_part(n, 2)
                    prod_low(n, 0)
                    exp_part(n, 3)
                    exp_part(n, 4)
                    q_times_sum(n, 1 - parity, 1)
                last_residual(g, 1)
                if ahead:
                    exp_part(n, 5)
                    prod_low(n, 1)
                a_low(g * GT + 1)
                if ahead:
                    exp_part(n, 6)
                    exp_part(n, 7)
                    q_times_sum(n, 1 - parity, 2)
                    prod_low(n, 2)
                if two_ahead:
                    rstd_of(g + 2)
                if ahead:
                    q_times_sum(n, 1 - parity, 3)
                last_residual(g, 2)
                if ahead:
                    prod_low(n, 3)
                a_low(g * GT + 2)
                last_residual(g, 3)
                a_low(g * GT + 3)

            groups(pool, 2, NG - 2, group)
            residual(NG * GT - 1, 1, NG * 2 - 1)

        @block.scalar
        def _(act):
            def xt_high(g, c):
                wait(act, xf_ready, g * C + c + 1)
                act.activation(xt_hi[:, c, :], xf[:, c % 2, :], ACT.Copy).then_inc(xt_hi_done, 1)

            def exp_relu(g, n):
                kind, c = unit_of(n)
                bias, scale = qk_bias[:, 1 - kind, c:c + 1], (1.0, Q_SCALE)[kind]
                wait(act, pj_ready, g * UNITS + n + 1)
                wait(act, phi_ready, g * 2 * C + n - 1)
                act.activation(z_exp[:, n % 2, :], pj[:, n % 2, :], ACT.Exp, bias=bias, scale=scale).then_inc(exp_ready, 1)
                act.activation(z_relu[:, n % 2, :], pj[:, n % 2, :], ACT.Relu, bias=bias, scale=scale).then_inc(relu_ready, 1)

            def prod_high(g, c):
                wait(act, prod_ready, g * C + c + 1)
                wait(act, den_ps, g * C + c)
                act.activation(prod_hi[:, :], prod[:, :], ACT.Copy).then_inc(prod_hi_ready, 1)

            def den_out(g, parity, c):
                wait(act, den_ps, g * C + c + 1)
                act.activation(r_den[parity][:, c, :], den_tp[:, :], ACT.Copy, bias=EPS_DEN).then_inc(den_ready, 1)

            def q_blocks(tile, g, parity, t):
                wait(act, phi_ready, (g + 1) * 2 * C)
                wait(act, sc_ready, tile * C)
                for h in range(HPC):
                    rows = slice(h * E, (h + 1) * E)
                    ins = act.activation(q_diag[rows, :, h, :], qt[parity][rows, :, t * P:(t + 1) * P], ACT.Copy)
                ins.then_inc(qdiag_ready, 1)

            def k_rows(tile, t):
                wait(act, kt_ps, tile + 1)
                wait(act, state_ready, tile - 1)
                act.activation(k_tok[:, t % 2, :], kt_op[:, :], ACT.Copy).then_inc(ktok_ready, 1)

            def a_high(tile):
                wait(act, a_ready, tile + 1)
                wait(act, op_ready, tile)
                act.activation(a_hi[:, :], a_t[:, :], ACT.Copy).then_inc(a_hi_ready, 1)

            def ffn_weights(t):
                for i in ((0, 1), (2, 3, 4), (5, 6, 7), ())[t]:
                    act.wait_ge(raw_in[i % RAW], 16 * (i // RAW + 1))
                    if i == 0:
                        act.wait_ge(pj_ready, NG * UNITS)
                    act.activation((w_hi if i < C else w_lo)[:, i % C, 0:HID], raw[i % RAW],
                                   ACT.Copy).then_inc(ffn_w_ready, 1)

            act.wait_ge(init_done, 1)
            for c in range(C):
                xt_high(0, c)
            for c in range(C):
                exp_relu(0, 2 * c)
                exp_relu(0, 2 * c + 1)
                prod_high(0, c)
                den_out(0, 0, c)
            for c in range(C):
                xt_high(1, c)
            q_blocks(0, 0, 0, 0)

            def group(g, parity):
                ahead = not isinstance(g, int) or g + 1 < NG
                two_ahead = not isinstance(g, int) or g + 2 <= NG
                n = g + 1
                other = 1 - parity
                last = isinstance(g, int) and g == NG - 1
                if ahead:
                    exp_relu(n, 0)
                    exp_relu(n, 1)
                k_rows(g * GT, 0)
                q_blocks(g * GT + 1, g, parity, 1)
                a_high(g * GT)
                if last:
                    ffn_weights(0)
                if ahead:
                    exp_relu(n, 2)
                    prod_high(n, 0)
                    exp_relu(n, 3)
                    exp_relu(n, 4)
                    exp_relu(n, 5)
                    den_out(n, other, 0)
                    prod_high(n, 1)
                k_rows(g * GT + 1, 1)
                q_blocks(g * GT + 2, g, parity, 2)
                a_high(g * GT + 1)
                if last:
                    ffn_weights(1)
                if ahead:
                    exp_relu(n, 6)
                    exp_relu(n, 7)
                    den_out(n, other, 1)
                    prod_high(n, 2)
                    den_out(n, other, 2)
                    prod_high(n, 3)
                k_rows(g * GT + 2, 2)
                q_blocks(g * GT + 3, g, parity, 3)
                a_high(g * GT + 2)
                if last:
                    ffn_weights(2)
                if ahead:
                    den_out(n, other, 3)
                    q_blocks(g * GT + 4, n, other, 0)
                if two_ahead:
                    xt_high(g + 2, 0)
                    xt_high(g + 2, 1)
                k_rows(g * GT + 3, 3)
                if two_ahead:
                    xt_high(g + 2, 2)
                a_high(g * GT + 3)
                if last:
                    ffn_weights(3)
                if two_ahead:
                    xt_high(g + 2, 3)

            groups(act, 2, NG - 2, group)

        @block.vector
        def _(dve):
            def norm_stats(g):
                wait(dve, x_in, 16 * (g + 1))
                for t in range(GT):
                    ins = dve.bn_stats(stats[:, t, :], xg[:, t, :])
                ins.then_inc(ln_chain, 1)

            def norm_var(g):
                wait(dve, ln_chain, 2 * g + 1)
                wait(dve, xn_ready, g)
                if not isinstance(g, int):
                    dve.sem_inc(dve_passed, 1)
                for t in range(GT):
                    ins = dve.bn_aggr(mean_var[:, t, :], stats[:, t, :])
                ins.then_inc(ln_chain, 1)
                wait(dve, ln_chain, 2 * g + 2)
                dve.tensor_scalar(var_eps[:, :], mean_var[:, :, 1], EPS_LN, None, ALU.add).then_inc(var_ready, 1)

            def norm_x(g):
                wait(dve, rstd_ready, g + 1)
                for t in range(GT):
                    ins = dve.tensor_scalar(xg[:, t, :], xg[:, t, :], mean_var[:, t, 0:1], rstd[:, t:t + 1],
                                            ALU.subtract, ALU.mult)
                ins.then_inc(xn_ready, 1)

            def xt_full(g, c):
                shift, scale = (SB, CB) if isinstance(g, int) and g == NG else (SA, CA)
                wait(dve, xt_ps, g * C + c + 1)
                if c < 2:
                    wait(dve, phi_ready, g * 2 * C)
                else:
                    wait(dve, xt_lo_done, g * C + c - 1)
                dve.tensor_scalar(xf[:, c % 2, :], turn_bank[c], mod_col[:, scale, c:c + 1],
                                  mod_col[:, shift, c:c + 1], ALU.mult, ALU.add).then_inc(xf_ready, 1)

            def xt_low(g, c):
                wait(dve, xt_hi_done, g * C + c + 1)
                dve.tensor_tensor(out=xt_lo[:, c, :], in0=xf[:, c % 2, :], in1=xt_hi[:, c, :].bitcast(F32),
                                  op=ALU.subtract).then_inc(xt_lo_done, 1)

            def x_by_feature(g):
                for c in range(C + 1):
                    if c < C:
                        xt_full(g, c)
                    if c > 0:
                        xt_low(g, c - 1)

            def feature(g, parity, n):
                kind, c = unit_of(n)
                to = (kt, qt)[kind][parity]
                wait(dve, emin_ready, g * 2 * C + n + 1)
                wait(dve, relu_ready, g * 2 * C + n + 1)
                dve.tensor_tensor(out=to[:, c, :], in0=z_exp[:, n % 2, :], in1=z_relu[:, n % 2, :],
                                  op=ALU.add).then_inc(phi_ready, 1)
                if kind == 0:
                    wait(dve, phi_ready, g * 2 * C + n + 1)
                    wait(dve, prod_ready, (g - 1) * C + c + 1)
                    first = isinstance(g, int) and g == 0
                    dve.tensor_tensor_scan(k_sum[:, c, :], to[:, c, :], to[:, c, :],
                                           0.0 if first else k_sum[:, c, GN - 1:GN],
                                           ALU.add, ALU.bypass).then_inc(ksum_ready, 1)

            def v_rows(g, parity, t):
                wait(dve, pj_ready, g * UNITS + 2 * C + t + 1)
                dve.tensor_tensor(out=v[parity][:, t, :], in0=pj[:, t % 2, :], in1=bv_row[:, :],
                                  op=ALU.add).then_inc(v_ready, 1)

            def recip(g, parity, c):
                wait(dve, den_ready, g * C + c + 1)
                dve.reciprocal(r_den[parity][:, c, :], r_den[parity][:, c, :]).then_inc(rden_ready, 1)

            def mask(tile, c):
                wait(dve, sc_ready, tile * C + c + 1)
                dve.tensor_tensor(out=probs[:, c, :].rearrange("p (h i) -> p h i", h=HPC),
                                  in0=sc[:, c % 2, :].rearrange("p (h i) -> p h i", h=HPC),
                                  in1=causal[:, :].rearrange("p (a i) -> p a i", a=1).broadcast_to([P, HPC, P]),
                                  op=ALU.mult).then_inc(probs_ready, 1)

            def divide(tile, g, parity, t):
                wait(dve, num_ready, tile + 1)
                wait(dve, rden_ready, (g + 1) * C)
                wait(dve, a_lo_ready, tile)
                dve.tensor_tensor(out=a_t[:, :].rearrange("p (c i) -> p c i", c=C),
                                  in0=num[:, :].rearrange("p (c i) -> p c i", c=C),
                                  in1=r_den[parity][:, :, t * P:(t + 1) * P], op=ALU.mult).then_inc(a_ready, 1)

            def state_out(tile):
                wait(dve, state_ready, tile + 1)
                dve.tensor_tensor(out=kv_diag[:, :, :], in0=state[:, :].rearrange("p (c f) -> p c f", c=C),
                                  in1=head_diag[:, :].rearrange("p (a f) -> p a f", a=1).broadcast_to([P, C, P]),
                                  op=ALU.mult).then_inc(kv_ready, 1)

            def gate_y(tile, slot, uses):
                wait(dve, op_ready, tile + 1)
                wait(dve, y_out[slot], 16 * uses)
                dve.tensor_tensor(out=y[:, slot, :], in0=kt_op[:, :], in1=ga_row[:, :],
                                  op=ALU.mult).then_inc(y_gated, 1)

            def gate_last(g, t):
                tile = g * GT + t - 1
                if not isinstance(tile, int) or tile >= 0:
                    gate_y(tile, (t + 1) % 2, g * 2 + (t - 1) // 2)

            def ffn_sizes(pieces):
                for i in pieces:
                    dve.wait_ge(raw_in[i % RAW], 16 * (i // RAW + 1))
                    dve.tensor_reduce(most[:, i:i + 1], raw[i % RAW], AX.X, ALU.max,
                                      apply_absolute_value=True).then_inc(most_ready, 1)

            dve.memset(ones[:, :], 1.0)
            dve.memset(q_diag[:, :, :, :], 0.0)
            dve.memset(kv_diag[:, :, :], 0.0).then_inc(init_done, 1)
            for g in range(2):
                norm_stats(g)
                norm_var(g)
                norm_x(g)
                if g == 0:
                    x_by_feature(0)
                    for n in range(2 * C):
                        feature(0, 0, n)
                    for t in range(GT):
                        v_rows(0, 0, t)
            recip(0, 0, 0)
            recip(0, 0, 1)
            recip(0, 0, 2)
            x_by_feature(1)

            def group(g, parity):
                ahead = not isinstance(g, int) or g + 1 < NG
                two_ahead = not isinstance(g, int) or g + 2 <= NG
                n = g + 1
                other = 1 - parity
                last = isinstance(g, int) and g == NG - 1
                for t in range(GT):
                    tile = g * GT + t
                    mask(tile, 0)
                    mask(tile, 1)
                    if t == 0:
                        recip(g, parity, 3)
                    elif ahead and t < 3:
                        feature(n, other, 4 * t - 1)
                        if t == 2:
                            recip(n, other, 0)
                    elif ahead:
                        recip(n, other, 2)
                        v_rows(n, other, 3)
                    gate_last(g, t)
                    mask(tile, 2)
                    mask(tile, 3)
                    if ahead and t < 2:
                        feature(n, other, 4 * t)
                        if two_ahead and t == 1:
                            norm_stats(g + 2)
                        feature(n, other, 4 * t + 1)
                    elif ahead and t == 2:
                        v_rows(n, other, 0)
                        v_rows(n, other, 1)
                        recip(n, other, 1)
                    elif two_ahead and t == 3:
                        xt_full(g + 2, 0)
                        xt_full(g + 2, 1)
                        xt_low(g + 2, 0)
                        xt_full(g + 2, 2)
                        xt_low(g + 2, 1)
                    if last:
                        ffn_sizes(((0,), (2, 3), (5, 6), (8, 9))[t])
                    divide(tile, g, parity, t)
                    if two_ahead and t == 3:
                        xt_full(g + 2, 3)
                        xt_low(g + 2, 2)
                    state_out(tile)
                    if two_ahead and t == 1:
                        norm_var(g + 2)
                    if ahead and t < 2:
                        feature(n, other, 4 * t + 2)
                    elif ahead and t == 2:
                        v_rows(n, other, 2)
                    elif two_ahead and t == 3:
                        xt_low(g + 2, 3)
                    if two_ahead and t == 2:
                        norm_x(g + 2)
                    if last:
                        ffn_sizes(((1,), (4,), (7,), (10, 11))[t])

            groups(dve, 2, NG - 2, group)
            dve.wait_ge(most_ready, 3 * C)
            dve.tensor_reduce(beyond[:, :], most[:, :], AX.X, ALU.max).then_inc(beyond_ready, 1)
            dve.wait_ge(beyond_ready, 1)
            dve.tensor_scalar(beyond[:, :], beyond[:, :], EXACT, None, ALU.is_gt).then_inc(beyond_ready, 1)
            gate_y(NG * GT - 1, 1, NG * 2 - 1)
            dve.wait_ge(beyond_ps, 1)
            dve.tensor_scalar(wide[:, :], pj[0:1, 0, 0:1], 0.5, None, ALU.is_gt).then_inc(wide_ready, 1)
            dve.wait_ge(wide_ready, 1)

        @block.tensor
        def _(pe):
            def x_turn(g, c):
                wait(pe, xn_ready, g + 1)
                if c == 0:
                    wait(pe, v_ready, (g - 1) * C + 3)
                elif c == 1:
                    wait(pe, den_ready, g * C)
                elif c == 2:
                    wait(pe, v_ready, g * C)
                else:
                    wait(pe, xf_ready, g * C + 2)
                for t in range(GT):
                    mm = pe.transpose(turn_bank[c][:, t * P:(t + 1) * P], xg[:, t, c * P:(c + 1) * P], ident[:, :])
                mm.then_inc(xt_ps, 1)

            def project(g, u):
                kind, c = unit_of(u)
                if u == 0:
                    wait(pe, xt_lo_done, (g + 1) * C)
                if u < 2:
                    pass
                elif u < 2 * C + 2:
                    wait(pe, relu_ready, g * 2 * C + u - 1)
                else:
                    wait(pe, v_ready, g * C + u - 2 * C - 1)
                to = pj[:, u % 2, :]
                passes = [(hi_w, hi_x, k) for hi_w, hi_x in ((1, 1), (1, 0), (0, 1)) for k in range(C)]
                for i, (hi_w, hi_x, k) in enumerate(passes):
                    w = w_hi if hi_w else w_lo
                    xt = xt_hi if hi_x else xt_lo
                    if kind == 2:
                        mm = pe.matmul(to, xt[:, k, c * P:(c + 1) * P], w[:, k, WV:WV + D],
                                       start=(i == 0), stop=(i == len(passes) - 1))
                    else:
                        at = (WK, WQ)[kind] + c * P
                        mm = pe.matmul(to, w[:, k, at:at + P], xt[:, k, :],
                                       start=(i == 0), stop=(i == len(passes) - 1))
                mm.then_inc(pj_ready, 1)

            def denominators(g, c):
                wait(pe, prod_lo_ready, g * C + c + 1)
                if c == 0:
                    wait(pe, xf_ready, (g + 1) * C)
                else:
                    wait(pe, den_ready, g * C + c)
                pe.matmul(den_tp[:, :], head_ones[:, :], prod_hi[:, :], start=True, stop=False)
                pe.matmul(den_tp[:, :], head_ones[:, :], prod_lo[:, :], start=False, stop=True).then_inc(den_ps, 1)

            def scores(tile, parity, t, c):
                if c == 0:
                    wait(pe, qdiag_ready, tile + 1)
                wait(pe, probs_ready, tile * C + c - 1)
                pe.matmul(sc[:, c % 2, :], kt[parity][:, c, t * P:(t + 1) * P],
                          q_diag[:, c, :, :].rearrange("p h i -> p (h i)"), start=True, stop=True).then_inc(sc_ready, 1)

            def k_turn(tile, parity, t):
                wait(pe, y_gated, tile)
                for c in range(C):
                    mm = pe.transpose(kt_op[:, c * P:(c + 1) * P], kt[parity][:, c, t * P:(t + 1) * P], ident[:, :])
                mm.then_inc(kt_ps, 1)

            def numerators(tile, g, parity, t):
                wait(pe, kv_ready, tile)
                wait(pe, a_ready, tile)
                for c in range(C):
                    pe.matmul(num[:, c * P:(c + 1) * P], kv_diag[:, c, :], qt[parity][:, c, t * P:(t + 1) * P],
                              start=(c == 0), stop=False, skip_group_check=True)
                wait(pe, v_ready, g * C + t + 1)
                for c in range(C):
                    wait(pe, probs_ready, tile * C + c + 1)
                    for h in range(HPC):
                        f = c * P + h * E
                        mm = pe.matmul(num[h * E:(h + 1) * E, c * P:(c + 1) * P], v[parity][:, t, f:f + E],
                                       probs[:, c, h * P:(h + 1) * P], start=False, stop=(c == C - 1),
                                       skip_group_check=True)
                mm.then_inc(num_ready, 1)

            def add_state(tile, parity, t):
                wait(pe, ktok_ready, tile + 1)
                for c in range(C):
                    f = slice(c * P, (c + 1) * P)
                    mm = pe.matmul(state[:, f], k_tok[:, t % 2, f], v[parity][:, t, f], start=False, stop=False,
                                   skip_group_check=True)
                mm.then_inc(state_ready, 1)

            def out_project(tile):
                wait(pe, a_lo_ready, tile + 1)
                wait(pe, ktok_ready, tile + 1)
                passes = [(a, w, c) for a, w in ((a_hi, w_hi), (a_hi, w_lo), (a_lo, w_hi)) for c in range(C)]
                for i, (a, w, c) in enumerate(passes):
                    mm = pe.matmul(kt_op[:, :], a[:, c * P:(c + 1) * P], w[:, c, WO:WO + D],
                                   start=(i == 0), stop=(i == len(passes) - 1))
                mm.then_inc(op_ready, 1)

            pe.wait_ge(init_done, 1)
            pe.matmul(state[:, :], kv_diag[:, 0, :], q_diag[:, 0, :, :].rearrange("p h i -> p (h i)"),
                      start=True, stop=False, skip_group_check=True)
            for c in range(C):
                x_turn(0, c)
            for u in range(UNITS):
                project(0, u)
                if u >= 3 and u % 2:
                    if (u - 3) // 2 < C:
                        denominators(0, (u - 3) // 2)
            for c in range(C):
                x_turn(1, c)

            def group(g, parity):
                ahead = not isinstance(g, int) or g + 1 < NG
                two_ahead = not isinstance(g, int) or g + 2 <= NG
                n = g + 1
                for t in range(GT):
                    tile = g * GT + t

                    def fill(i):
                        if 4 * t + i < UNITS - 1 and ahead:
                            project(n, 4 * t + i)
                        elif t == 3:
                            if i == 0 and ahead:
                                project(n, UNITS - 1)
                            if two_ahead:
                                for c in ((), (0, 1, 2), (3,), ())[i]:
                                    x_turn(g + 2, c)

                    scores(tile, parity, t, 0)
                    scores(tile, parity, t, 1)
                    if t == 0 and (not isinstance(tile, int) or tile > 0):
                        out_project(tile - 1)
                    fill(0)
                    if t == 1 and ahead:
                        denominators(n, 0)
                    if t > 0:
                        out_project(tile - 1)
                    scores(tile, parity, t, 2)
                    scores(tile, parity, t, 3)
                    fill(1)
                    if t == 2 and ahead:
                        denominators(n, 2)
                    k_turn(tile, parity, t)
                    numerators(tile, g, parity, t)
                    fill(2)
                    if t == 1 and ahead:
                        denominators(n, 1)
                    add_state(tile, parity, t)
                    fill(3)
                    if t == 2 and ahead:
                        denominators(n, 3)

            groups(pe, 2, NG - 2, group)
            out_project(NG * GT - 1)
            pe.wait_ge(beyond_ready, 2)
            pe.matmul(pj[0:1, 0, 0:1], beyond[:, :], ones[:, :], start=True, stop=True).then_inc(beyond_ps, 1)


def feed_forward(nc, sem, sbuf, psum, ident, mod_col, half_neg, w_hi, w_lo, xt_hi0, xt_lo0, wide, gb_row,
                 w_gate_t, w_up_t, w_down_t, x_mid, out):
    with ExitStack() as s:
        xg = [sbuf(s, f"fx{i}", [P, GT, D]) for i in range(2)]
        xn = sbuf(s, "fxn", [P, GT, D])
        stats = sbuf(s, "fstats", [P, GT, 6])
        mean_var = sbuf(s, "fmean_var", [P, GT, 2])
        var_eps = sbuf(s, "fvar_eps", [P, GT])
        rstd = sbuf(s, "frstd", [P, GT])
        xt_hi = [xt_hi0, sbuf(s, "fxt_hi1", [P, C, GN], F32R)]
        xt_lo = [xt_lo0, sbuf(s, "fxt_lo1", [P, C, GN], F32R)]
        xf = sbuf(s, "fxf", [P, 2, GN])
        wg, wu = w_hi, w_lo
        wd = sbuf(s, "wd", [P, HB, D], F32R)
        gate = sbuf(s, "gate", [P, 2, GN])
        h = sbuf(s, "h", [P, 2, GN])
        h_hi = sbuf(s, "h_hi", [P, HB, GN], F32R)
        h_lo = sbuf(s, "h_lo", [P, HB, GN], F32R)
        y = sbuf(s, "fy", [P, 2, D])
        gu = psum(s, "gu", [P, 4, 512])
        tp = psum(s, "tp", [P, 2, 512])
        dn = psum(s, "dn", [P, 2, 512])

        x_in, y_out = [sem(f"fx_in{i}") for i in range(2)], [sem(f"fy_out{i}") for i in range(2)]
        ln_chain, var_ready, rstd_ready, xn_ready = (sem("fln_chain"), sem("fvar_ready"), sem("frstd_ready"),
                                                     sem("fxn_ready"))
        xt_ps, xf_ready, xt_hi_done, xt_lo_done = sem("fxt_ps"), sem("fxf_ready"), sem("fxt_hi_done"), sem("fxt_lo_done")
        down_in, wd_ready = [sem(f"down_in{i}") for i in range(2)], sem("wd_ready")
        int_in, word_ready, w_moved = sem("int_in"), sem("word_ready"), sem("w_moved")
        gate_ps, up_ps, gate_ready, h_ready, h_hi_ready, h_lo_ready = (
            sem("gate_ps"), sem("up_ps"), sem("gate_ready"), sem("h_ready"), sem("h_hi_ready"), sem("h_lo_ready"))
        dn_ps, y_gated, y_ready, dve_passed = sem("dn_ps"), sem("fy_gated"), sem("fy_ready"), sem("fdve_passed")

        mid_groups = x_mid.rearrange("(g t p) d -> g p t d", t=GT, p=P)
        out_tiles = out.rearrange("a (t p) d -> (a t) p d", p=P)

        down_chunks = w_down_t.rearrange("(j p) n -> j p n", p=P)
        down_raw = [y[:, i, :].bitcast(I32) for i in range(2)]

        block = s.enter_context(nc.Block())

        @block.sync
        def _(sp):
            def load(g, parity):
                wait(sp, y_ready, (g - 1) * GT)
                sp.dma_start(xg[parity][:, :, :], mid_groups[g, :, :, :] if isinstance(g, int) else
                             mid_groups[bass.ds(g, 1), :, :, :].rearrange("a p t d -> (a p) t d")).then_inc(x_in[parity], 16)

            for j in range(HB):
                wait(sp, wd_ready, j - 1)
                sp.dma_start(down_raw[j % 2], down_chunks[j, :, :]).then_inc(down_in[j % 2], 16)
                if j == 1:
                    load(1, 1)
            load(0, 0)

            def group(g, parity):
                if isinstance(g, int) and g == 0:
                    pass
                elif not isinstance(g, int) or g + 1 < NG:
                    load(g + 1, 1 - parity)
                for t in range(GT):
                    tile = g * GT + t
                    wait(sp, y_ready, tile + 1)
                    sp.dma_start(out_tiles[tile, :, :] if isinstance(tile, int) else
                                 out_tiles[bass.ds(tile, 1), :, :].rearrange("a p d -> (a p) d"),
                                 y[:, t % 2, :]).then_inc(y_out[t % 2], 16)

            groups(sp, 2, NG - 2, group)
            for slot in range(2):
                sp.wait_ge(y_out[slot], 16 * NG * GT // 2)

        @block.gpsimd
        def _(pool):
            def rstd_of(g):
                wait(pool, var_ready, g)
                pool.tensor_tensor(out=rstd[:, :], in0=var_eps[:, :], in1=half_neg[:, :], op=ALU.pow).then_inc(rstd_ready, 1)

            def h_low(g, j):
                wait(pool, h_hi_ready, g * HB + j + 1)
                pool.tensor_tensor(out=h_lo[:, j, :], in0=h[:, j % 2, :], in1=h_hi[:, j, :].bitcast(F32),
                                   op=ALU.subtract).then_inc(h_lo_ready, 1)

            def group(g, parity):
                for j in range(HB):
                    h_low(g, j)
                    if j == 1 and (not isinstance(g, int) or g + 1 < NG):
                        rstd_of(g + 1)
                if isinstance(g, int) and g == 0:
                    pool.wait_ge(x_in[0], 16)
                for t in range(GT):
                    wait(pool, y_gated, g * GT + t + 1)
                    pool.tensor_tensor(out=y[:, t % 2, :], in0=y[:, t % 2, :], in1=xg[parity][:, t, :],
                                       op=ALU.add).then_inc(y_ready, 1)

            groups(pool, 2, NG - 2, group)

        def words(act, src, to, done):
            act.dma_start(h[:, 0, :].bitcast(I32), src).then_inc(int_in, 16)
            act.wait_ge(int_in, 16 * (done + 1))
            act.activation(gate[:, 0, :], h[:, 0, :].bitcast(I32), ACT.Copy).then_inc(word_ready, 1)
            act.wait_ge(word_ready, done + 1)
            act.dma_start(to.bitcast(F32), gate[:, 0, :]).then_inc(w_moved, 16)
            act.wait_ge(w_moved, 16 * (done + 1))

        @block.scalar
        def _(act):
            def xt_high(g, parity, c):
                wait(act, xt_ps, (g - 1) * C + c + 1)
                wait(act, xt_lo_done, (g - 1) * C + c - 1)
                act.activation(xf[:, c % 2, :], tp[:, c % 2, :], ACT.Identity, bias=mod_col[:, SB, c:c + 1],
                               scale=mod_col[:, CB, c:c + 1]).then_inc(xf_ready, 1)
                wait(act, xf_ready, (g - 1) * C + c + 1)
                act.activation(xt_hi[parity][:, c, :], xf[:, c % 2, :], ACT.Copy).then_inc(xt_hi_done, 1)

            flag = act.value_load(wide[0:1, 0:1])
            with act.If(flag > 0):
                done = 0
                for w, src in ((wg, w_gate_t), (wu, w_up_t)):
                    for k in range(C):
                        for b in range(HID // D):
                            cols = slice(b * D, (b + 1) * D)
                            words(act, src[k * P:(k + 1) * P, cols], w[:, k, cols], done)
                            done += 1
                for j in range(HB):
                    act.wait_ge(down_in[j % 2], 16 * (j // 2 + 1))
                    act.activation(gate[:, 0, :], down_raw[j % 2], ACT.Copy).then_inc(word_ready, 1)
                    done += 1
                    act.wait_ge(word_ready, done)
                    act.dma_start(wd[:, j, :].bitcast(F32), gate[:, 0, :]).then_inc(w_moved, 16)
                    act.wait_ge(w_moved, 16 * done)
                    act.sem_inc(wd_ready, 1)

            def down_weights(js):
                with act.If(flag < 1):
                    for j in js:
                        act.wait_ge(down_in[j % 2], 16 * (j // 2 + 1))
                        act.activation(wd[:, j, :], down_raw[j % 2], ACT.Copy).then_inc(wd_ready, 1)

            def group(g, parity):
                for j in range(HB):
                    n = g * HB + j
                    wait(act, gate_ps, n + 1)
                    wait(act, h_ready, n - 1)
                    act.activation(gate[:, j % 2, :], gu[:, 2 * (j % 2), :], ACT.Silu,
                                   scale=W_SCALE).then_inc(gate_ready, 1)
                    wait(act, h_ready, n + 1)
                    act.activation(h_hi[:, j, :], h[:, j % 2, :], ACT.Copy).then_inc(h_hi_ready, 1)
                    if isinstance(g, int) and g == 0 and j < HB // 2:
                        down_weights((2 * j, 2 * j + 1))
                    if j >= 4 and j < 8 and (not isinstance(g, int) or g + 1 < NG):
                        xt_high(g + 1, 1 - parity, j - 4)

            groups(act, 2, NG - 2, group)

        @block.vector
        def _(dve):
            def norm_stats(g, parity):
                wait(dve, x_in[parity], 16 * (g // 2 + 1) if isinstance(g, int) else g * 8 + (16 - 8 * parity))
                wait(dve, ln_chain, 2 * (g - 1))
                for t in range(GT):
                    ins = dve.bn_stats(stats[:, t, :], xg[parity][:, t, :])
                ins.then_inc(ln_chain, 1)
                wait(dve, ln_chain, 2 * (g - 1) + 1)
                wait(dve, xn_ready, g - 1)
                if not isinstance(g, int):
                    dve.sem_inc(dve_passed, 1)
                for t in range(GT):
                    ins = dve.bn_aggr(mean_var[:, t, :], stats[:, t, :])
                ins.then_inc(ln_chain, 1)
                wait(dve, ln_chain, 2 * g)
                dve.tensor_scalar(var_eps[:, :], mean_var[:, :, 1], EPS_LN, None, ALU.add).then_inc(var_ready, 1)

            def norm_x(g, parity):
                wait(dve, rstd_ready, g)
                wait(dve, xt_ps, (g - 1) * C)
                for t in range(GT):
                    ins = dve.tensor_scalar(xn[:, t, :], xg[parity][:, t, :], mean_var[:, t, 0:1], rstd[:, t:t + 1],
                                            ALU.subtract, ALU.mult)
                ins.then_inc(xn_ready, 1)

            def xt_low(g, parity, c):
                wait(dve, xt_hi_done, (g - 1) * C + c + 1)
                dve.tensor_tensor(out=xt_lo[parity][:, c, :], in0=xf[:, c % 2, :], in1=xt_hi[parity][:, c, :].bitcast(F32),
                                  op=ALU.subtract).then_inc(xt_lo_done, 1)

            def group(g, parity):
                ahead = not isinstance(g, int) or g + 1 < NG
                for j in range(HB):
                    n = g * HB + j
                    wait(dve, up_ps, n + 1)
                    wait(dve, gate_ready, n + 1)
                    wait(dve, h_lo_ready, n - 1)
                    dve.tensor_tensor(out=h[:, j % 2, :], in0=gu[:, 2 * (j % 2) + 1, :], in1=gate[:, j % 2, :],
                                      op=ALU.mult).then_inc(h_ready, 1)
                    if ahead and j == 0:
                        norm_stats(g + 1, 1 - parity)
                    if ahead and j == 2:
                        norm_x(g + 1, 1 - parity)
                    if ahead and 4 <= j < 8:
                        xt_low(g + 1, 1 - parity, j - 4)
                for t in range(GT):
                    wait(dve, dn_ps, g * GT + t + 1)
                    wait(dve, y_out[t % 2], g * 32 + 16 * (t // 2))
                    dve.tensor_tensor(out=y[:, t % 2, :], in0=dn[:, t % 2, :], in1=gb_row[:, :],
                                      op=ALU.mult).then_inc(y_gated, 1)

            groups(dve, 2, NG - 2, group)

        @block.tensor
        def _(pe):
            def x_turn(g, c):
                wait(pe, xn_ready, g)
                wait(pe, xf_ready, (g - 1) * C + c - 1)
                for t in range(GT):
                    mm = pe.transpose(tp[:, c % 2, t * P:(t + 1) * P], xn[:, t, c * P:(c + 1) * P], ident[:, :])
                mm.then_inc(xt_ps, 1)

            def passes(exact):
                return (lambda ap: ap) if exact else (lambda ap: ap.bitcast(F32))

            def all_groups(exact):
                as_ = passes(exact)

                def hidden(g, parity, j, w, bank, done):
                    for i, (xt, k) in enumerate((xt, k) for xt in (xt_hi, xt_lo) for k in range(C)):
                        mm = pe.matmul(gu[:, bank, :], as_(w[:, k, j * P:(j + 1) * P]), as_(xt[parity][:, k, :]),
                                       start=(i == 0), stop=(i == 2 * C - 1))
                    mm.then_inc(done, 1)

                def down(g, t):
                    wait(pe, y_gated, g * GT + t - 1)
                    for j in range(HB):
                        if t == 0:
                            wait(pe, h_lo_ready, g * HB + j + 1)
                            if isinstance(g, int) and g == 0:
                                pe.wait_ge(wd_ready, j + 1)
                        for half in (h_hi, h_lo):
                            mm = pe.matmul(dn[:, t % 2, :], as_(half[:, j, t * P:(t + 1) * P]), as_(wd[:, j, :]),
                                           start=(j == 0 and half is h_hi), stop=(j == HB - 1 and half is h_lo))
                    mm.then_inc(dn_ps, 1)

                def group(g, parity):
                    wait(pe, xt_lo_done, g * C)
                    for j in range(HB):
                        n = g * HB + j
                        wait(pe, gate_ready, n - 1)
                        hidden(g, parity, j, wg, 2 * (j % 2), gate_ps)
                        wait(pe, h_ready, n - 1)
                        hidden(g, parity, j, wu, 2 * (j % 2) + 1, up_ps)
                        if 4 <= j < 8 and (not isinstance(g, int) or g + 1 < NG):
                            x_turn(g + 1, j - 4)
                    for t in range(GT):
                        down(g, t)

                groups(pe, 2, NG - 2, group)

            flag = pe.value_load(wide[0:1, 0:1])
            with pe.If(flag > 0):
                pe.wait_ge(w_moved, 16 * 3 * HB)
                all_groups(False)
            with pe.Else():
                all_groups(True)


_INS = ["L0_attn_x", "L0_attn_W_qkv", "L0_attn_b_qkv", "L0_attn_W_out", "L0_attn_b_out",
        "L0_ffn_w_gate", "L0_ffn_w_up", "L0_ffn_w_down", "L0_c", "L0_wmod"]
_TURNED = ("L0_ffn_w_gate", "L0_ffn_w_up", "L0_ffn_w_down", "L0_c")


def kernel(**inputs):
    import concourse.bacc as bacc
    from concourse.bass_utils import run_bass_kernel_spmd

    nc = bacc.Bacc("TRN2", target_bir_lowering=False, num_devices=1, dynamic_dma_scratch_size=1024)
    arrays, args = {}, []
    for name in _INS:
        a = np.asarray(inputs[name])
        if name == "L0_c":
            a = a.reshape(C, P)
        layouts = [(f"in_{name}", a.T if name in _TURNED else a)]
        if name == "L0_attn_b_qkv":
            layouts.append(("in_b_cols", a.reshape(3 * C, P).T))
        for label, a in layouts:
            arrays[label] = np.ascontiguousarray(a)
            args.append(nc.dram_tensor(label, a.shape, mybir.dt.from_np(a.dtype), kind="ExternalInput").ap())
    out = nc.dram_tensor("out", (1, L, D), F32, kind="ExternalOutput").ap()
    build(nc, *args, out)
    r = run_bass_kernel_spmd(nc, [arrays], core_ids=[0])
    return r.results[0]["out"]
```

```python
from contextlib import ExitStack

import numpy as np

import concourse.bass as bass
from concourse import mybir

F32 = mybir.dt.float32
F32R = mybir.dt.float32r
I32 = mybir.dt.int32
ALU = mybir.AluOpType
ACT = mybir.ActivationFunctionType
AX = mybir.AxisListType

P = 128
L = 8192
D = 512
HID = 1536
E = 32
C = D // P
HB = HID // P
HPC = P // E
GT = 4
GN = GT * P
NG = L // GN
UNITS = 3 * C
SPLIT = C // 2
EPS_LN = 1e-5
EPS_FEAT = 1e-4
EPS_DEN = 1e-6
Q_SCALE = float(E) ** -0.5
EXACT = 4096.0
SA, CA, SB, CB = range(4)
SA_MOD, CA_MOD, GA_MOD, SB_MOD, CB_MOD, GB_MOD = range(6)
W_SCALE = float(np.float32(1.0 / 127.0))


def wait(eng, sem, value):
    if not isinstance(value, int) or value > 0:
        eng.wait_ge(sem, value)


def groups(eng, first, last, body):
    for g in range(first):
        body(g, g % 2)
    with eng.Fori(first // 2, last // 2) as pair:
        for parity in range(2):
            body(pair * 2 + parity, parity)
    for g in range(last, NG):
        body(g, g % 2)


def build(nc, x, w_qkv, b_qkv, b_cols, w_out, b_out, w_gate_t, w_up_t, w_down_t, c_vec, w_mod, out):
    top = ExitStack()
    with top:
        def sem(name):
            return top.enter_context(nc.semaphore(name))

        def sbuf(stack, name, shape, dt=F32):
            return stack.enter_context(nc.sbuf_tensor(name, shape, dt))

        def psum(stack, name, shape):
            return stack.enter_context(nc.psum_tensor(name, shape, F32))

        x_mid = nc.dram_tensor("x_mid", (L, D), F32, kind="Internal").ap()
        gb_dram = nc.dram_tensor("gb_dram", (1, D), F32, kind="Internal").ap()

        ident = sbuf(top, "ident", [P, P])
        mod_col = sbuf(top, "mod_col", [P, 4, C])
        half_neg = sbuf(top, "half_neg", [P, GT])
        wide = sbuf(top, "wide", [1, 1], I32)
        w_hi = sbuf(top, "w_hi", [P, C, 4 * D], F32R)
        w_lo = sbuf(top, "w_lo", [P, C, 4 * D], F32R)
        xt_hi = sbuf(top, "xt_hi", [P, C, GN], F32R)
        xt_lo = sbuf(top, "xt_lo", [P, C, GN], F32R)

        with ExitStack() as attn:
            ga_row = sbuf(attn, "ga_row", [P, D])
            gabo_row = sbuf(attn, "gabo_row", [P, D])
            bv_row = sbuf(attn, "bv_row", [P, D])
            qk_bias = sbuf(attn, "qk_bias", [P, 2, C])
            causal = sbuf(attn, "causal", [P, P])
            head_diag = sbuf(attn, "head_diag", [P, P])
            head_ones = sbuf(attn, "head_ones", [P, P], F32R)
            c_col = sbuf(attn, "c_col", [P, C])
            xg = sbuf(attn, "xg", [P, GT, D])
            stats = sbuf(attn, "stats", [P, GT, 6])
            mean_var = sbuf(attn, "mean_var", [P, GT, 2])
            var_eps = sbuf(attn, "var_eps", [P, GT])
            rstd = sbuf(attn, "rstd", [P, GT])
            norm = (xg, stats, mean_var, var_eps, rstd, sem("x_in"), sem("ln_chain"), sem("var_ready"),
                    sem("rstd_ready"), sem("xn_ready"))
            setup(nc, sem, sbuf, psum, ident, mod_col, half_neg, w_hi, w_lo, bv_row, qk_bias, causal, head_diag,
                  head_ones, c_col, norm, x, w_qkv, b_qkv, b_cols, w_out, c_vec, w_mod)
            attention(nc, sem, sbuf, psum, ident, gb_dram, mod_col, half_neg, w_hi, w_lo, xt_hi, xt_lo, ga_row,
                      gabo_row, bv_row, qk_bias, causal, head_ones, c_col, norm, wide, x, b_out, w_mod,
                      w_gate_t, w_up_t, w_down_t, x_mid)
        feed_forward(nc, sem, sbuf, psum, ident, mod_col, half_neg, w_hi, w_lo, xt_hi, xt_lo, wide, gb_dram,
                     w_gate_t, w_up_t, w_down_t, x_mid, out)


def modulation_column(pe, bank, wm, c_col):
    for c in range(C):
        for k in range(C):
            mm = pe.matmul(bank[:, c:c + 1], wm[:, k, c * P:(c + 1) * P], c_col[:, k:k + 1],
                           start=(k == 0), stop=(k == C - 1))
    return mm


def setup(nc, sem, sbuf, psum, ident, mod_col, half_neg, w_hi, w_lo, bv_row, qk_bias, causal, head_diag,
          head_ones, c_col, norm, x, w_qkv, b_qkv, b_cols, w_out, c_vec, w_mod):
    xg, stats, mean_var, var_eps, rstd, x_in, ln_chain, var_ready, rstd_ready, xn_ready = norm
    with ExitStack() as s:
        w_raw = sbuf(s, "w_raw", [P, C, 4 * D])
        wm = sbuf(s, "wm", [P, 2, C, D])
        c_exp = sbuf(s, "c_exp", [P, C])
        banks = psum(s, "setup_banks", [P, 2, 512])

        c_in, b_in = sem("c_in"), sem("b_in")
        w_in = [sem(f"w_in{k}") for k in range(C)]
        wm_in = [sem(f"wm_in{m}") for m in range(2)]
        const_done, pool_chain, c_neg_exp = sem("const_done"), sem("pool_chain"), sem("c_neg_exp")
        dve_chain, c_ready, mod_mm, hi_done = sem("setup_dve_chain"), sem("c_ready"), sem("mod_mm"), sem("hi_done")

        with nc.Block() as block:
            @block.sync
            def _(sp):
                sp.dma_start(c_col[:, :], c_vec).then_inc(c_in, 16)
                sp.dma_start(xg[:, :, :], x[0, 0:GN, :].rearrange("(t p) d -> p t d", p=P)).then_inc(x_in, 16)
                for i, m in enumerate((SA_MOD, CA_MOD)):
                    sp.dma_start(wm[:, i, :, :],
                                 w_mod[:, m * D:(m + 1) * D].rearrange("(c p) n -> p c n", p=P)).then_inc(wm_in[i], 16)

            @block.gpsimd
            def _(pool):
                pool.memset(ident[:, :], 0.0).then_inc(pool_chain, 1)
                pool.memset(causal[:, :], 1.0).then_inc(pool_chain, 1)
                pool.wait_ge(pool_chain, 2)
                pool.affine_select(out=ident[:, :], in_=ident[:, :], compare_op=ALU.not_equal, fill=1.0,
                                   base=0, pattern=[[-1, P]], channel_multiplier=1).then_inc(const_done, 1)
                pool.affine_select(out=causal[:, :], in_=causal[:, :], compare_op=ALU.is_ge, fill=0.0,
                                   base=0, pattern=[[1, P]], channel_multiplier=-1).then_inc(const_done, 1)
                pool.wait_ge(var_ready, 1)
                pool.tensor_tensor(out=rstd[:, :], in0=var_eps[:, :], in1=half_neg[:, :], op=ALU.pow).then_inc(rstd_ready, 1)

            @block.scalar
            def _(act):
                for k in range(C):
                    rows = slice(k * P, (k + 1) * P)
                    act.dma_start(w_raw[:, k, 0:3 * D], w_qkv[rows, :]).then_inc(w_in[k], 16)
                    act.dma_start(w_raw[:, k, 3 * D:4 * D], w_out[rows, :]).then_inc(w_in[k], 16)
                act.dma_start(qk_bias[:, :, :].rearrange("p a c -> p (a c)"), b_cols[:, 0:2 * C]).then_inc(b_in, 16)
                act.dma_start(bv_row[:, :], b_qkv[2 * D:3 * D].rearrange("(a n) -> a n", a=1).broadcast_to([P, D])).then_inc(b_in, 16)
                act.wait_ge(c_in, 16)
                act.activation(c_exp[:, :], c_col[:, :], ACT.Exp, scale=-1.0).then_inc(c_neg_exp, 1)
                for k in range(C):
                    act.wait_ge(w_in[k], 32)
                    act.activation(w_hi[:, k, :], w_raw[:, k, :], ACT.Copy).then_inc(hi_done, 1)

            @block.vector
            def _(dve):
                chain = [0]

                def link(ins):
                    chain[0] += 1
                    ins.then_inc(dve_chain, 1)
                    dve.wait_ge(dve_chain, chain[0])

                dve.memset(half_neg[:, :], -0.5)
                link(dve.memset(head_diag[:, :], 0.0))
                for h in range(HPC):
                    ins = dve.memset(head_diag[h * E:(h + 1) * E, h * E:(h + 1) * E], 1.0)
                link(ins)
                dve.tensor_copy(head_ones[:, :], head_diag[:, :])
                dve.wait_ge(c_neg_exp, 1)
                link(dve.tensor_scalar(c_exp[:, :], c_exp[:, :], 1.0, None, ALU.add))
                link(dve.reciprocal(c_exp[:, :], c_exp[:, :]))
                dve.tensor_tensor(out=c_col[:, :], in0=c_col[:, :], in1=c_exp[:, :], op=ALU.mult).then_inc(c_ready, 1)
                dve.wait_ge(x_in, 16)
                for t in range(GT):
                    ins = dve.bn_stats(stats[:, t, :], xg[:, t, :])
                ins.then_inc(ln_chain, 1)
                dve.wait_ge(ln_chain, 1)
                for t in range(GT):
                    ins = dve.bn_aggr(mean_var[:, t, :], stats[:, t, :])
                ins.then_inc(ln_chain, 1)
                dve.wait_ge(ln_chain, 2)
                dve.tensor_scalar(var_eps[:, :], mean_var[:, :, 1], EPS_LN, None, ALU.add).then_inc(var_ready, 1)
                dve.wait_ge(rstd_ready, 1)
                for t in range(GT):
                    ins = dve.tensor_scalar(xg[:, t, :], xg[:, t, :], mean_var[:, t, 0:1], rstd[:, t:t + 1],
                                            ALU.subtract, ALU.mult)
                ins.then_inc(xn_ready, 1)
                dve.wait_ge(mod_mm, 1)
                dve.tensor_copy(mod_col[:, SA, :], banks[:, 0, 0:C])
                dve.wait_ge(mod_mm, 2)
                dve.tensor_scalar(mod_col[:, CA, :], banks[:, 1, 0:C], 1.0, None, ALU.add)
                dve.wait_ge(b_in, 32)
                dve.tensor_scalar(qk_bias[:, 0, :], qk_bias[:, 0, :], Q_SCALE, None, ALU.mult)
                for k in range(C):
                    dve.wait_ge(hi_done, k + 1)
                    dve.tensor_tensor(out=w_lo[:, k, :], in0=w_raw[:, k, :], in1=w_hi[:, k, :].bitcast(F32),
                                      op=ALU.subtract)

            @block.tensor
            def _(pe):
                pe.wait_ge(c_ready, 1)
                for i in range(2):
                    pe.wait_ge(wm_in[i], 16)
                    modulation_column(pe, banks[:, i, :], wm[:, i, :, :], c_col).then_inc(mod_mm, 1)


def ffn_pieces(w_gate_t, w_up_t, w_down_t):
    pieces = [w[k * P:(k + 1) * P, :] for w in (w_gate_t, w_up_t) for k in range(C)]
    return pieces + [w_down_t[k * 3 * P:(k + 1) * 3 * P, :].rearrange("(h p) n -> p h n", p=P) for k in range(C)]


def attention(nc, sem, sbuf, psum, ident, gb_dram, mod_col, half_neg, w_hi, w_lo, xt_hi, xt_lo, ga_row,
              gabo_row, bv_row, qk_bias, causal, head_ones, c_col, norm, wide, x, b_out, w_mod,
              w_gate_t, w_up_t, w_down_t, x_mid):
    WQ, WK, WV, WO = 0, D, 2 * D, 3 * D
    xg, stats, mean_var, var_eps, rstd, x_in, ln_chain, var_ready, rstd_ready, xn_ready = norm
    with ExitStack() as s:
        z_exp = sbuf(s, "z_exp", [P, 2, GN])
        z_relu = sbuf(s, "z_relu", [P, 2, GN])
        xf = z_relu
        qt = [sbuf(s, f"qt{i}", [P, C, GN]) for i in range(2)]
        kt = [sbuf(s, f"kt{i}", [P, C, GN]) for i in range(2)]
        v = [sbuf(s, f"v{i}", [P, GT, D]) for i in range(2)]
        k_sum = sbuf(s, "k_sum", [P, 2, GN])
        k_past = sbuf(s, "k_past", [P, C])
        prod = sbuf(s, "prod", [P, GN])
        prod_hi = sbuf(s, "prod_hi", [P, GN], F32R)
        prod_lo = sbuf(s, "prod_lo", [P, GN], F32R)
        r_den = [sbuf(s, f"r_den{i}", [P, C, GN]) for i in range(2)]
        q_diag = sbuf(s, "q_diag", [P, SPLIT, HPC, P])
        k_pair = sbuf(s, "k_pair", [P, C - SPLIT, 2, P], F32R)
        q_high = sbuf(s, "q_high", [P, C - SPLIT, HPC, P], F32R)
        q_low = sbuf(s, "q_low", [P, C - SPLIT, HPC, P], F32R)
        probs = sbuf(s, "probs", [P, C, HPC * P])
        kv_diag = sbuf(s, "kv_diag", [P, C, P])
        k_tok = sbuf(s, "k_tok", [P, D])
        a_t = sbuf(s, "a_t", [P, D])
        a_hi = sbuf(s, "a_hi", [P, D], F32R)
        a_lo = sbuf(s, "a_lo", [P, D], F32R)
        x_res = sbuf(s, "x_res", [P, 2, D])
        y = sbuf(s, "y", [P, D])
        ones = sbuf(s, "ones_col", [P, 1])
        most = sbuf(s, "most", [P, 3 * C])
        beyond = sbuf(s, "beyond", [P, 1])
        pj = psum(s, "pj", [P, 2, 512])
        sc = psum(s, "sc", [P, 2, 512])
        num = psum(s, "num", [P, 512])
        state = psum(s, "state", [P, 512])
        den_tp = psum(s, "den_tp", [P, 512])
        kt_op = psum(s, "kt_op", [P, 512])
        turn_bank = [pj[:, 0, :], den_tp[:, :], pj[:, 1, :], den_tp[:, :]]

        init_done, pool_passed, dve_passed = sem("init_done"), sem("pool_passed"), sem("dve_passed")
        xr_in, y_out = [sem(f"xr_in{i}") for i in range(2)], [sem(f"y_out{i}") for i in range(2)]
        bo_in, wm_late_in, c_bc_ready, late_mm, late_chain = (
            sem("bo_in"), [sem(f"wm_late_in{i}") for i in range(4)], sem("c_bc_ready"), sem("late_mm"), sem("late_chain"))
        xt_ps, xf_ready, xt_hi_done, xt_lo_done = sem("xt_ps"), sem("xf_ready"), sem("xt_hi_done"), sem("xt_lo_done")
        raw_in = [sem(f"raw_in{i}") for i in range(5)]
        ffn_w_ready, most_ready, beyond_ready, beyond_ps, wide_ready = (
            sem("ffn_w_ready"), sem("most_ready"), sem("beyond_ready"), sem("beyond_ps"), sem("wide_ready"))
        pj_ready, exp_ready, relu_ready, emin_ready, phi_ready = (sem("pj_ready"), sem("exp_ready"), sem("relu_ready"),
                                                                  sem("emin_ready"), sem("phi_ready"))
        v_ready, ksum_ready, prod_ready, prod_hi_ready, prod_lo_ready = (
            sem("v_ready"), sem("ksum_ready"), sem("prod_ready"), sem("prod_hi_ready"), sem("prod_lo_ready"))
        past_ready, gb_ready, gb_saved = sem("past_ready"), sem("gb_ready"), sem("gb_saved")
        den_ps, den_ready, rden_ready = sem("den_ps"), sem("den_ready"), sem("rden_ready")
        diag_ready, own_ready, other_ready, low_ready, sc_ready, probs_ready = (
            sem("diag_ready"), sem("own_ready"), sem("other_ready"), sem("low_ready"), sem("sc_ready"), sem("probs_ready"))
        num_ready, a_ready, a_hi_ready, a_lo_ready = sem("num_ready"), sem("a_ready"), sem("a_hi_ready"), sem("a_lo_ready")
        kt_ps, ktok_ready, state_ready, kv_ready = sem("kt_ps"), sem("ktok_ready"), sem("state_ready"), sem("kv_ready")
        op_ready, y_gated, xr_ready, y_ready = sem("op_ready"), sem("y_gated"), sem("xr_ready"), sem("y_ready")

        x_groups = x.rearrange("a (g t p) d -> (a g) p t d", t=GT, p=P)
        x_tiles = x.rearrange("a (t p) d -> (a t) p d", p=P)
        mid_tiles = x_mid.rearrange("(t p) d -> t p d", p=P)
        mid_groups = x_mid.rearrange("(g t p) d -> g p t d", t=GT, p=P)
        raw = [buf[:, :, :].rearrange("p c n -> p (c n)")[:, 0:HID].bitcast(I32)
               for buf in (xg, qt[0], kt[0], v[0], r_den[0])]
        RAW = len(raw)
        pieces = ffn_pieces(w_gate_t, w_up_t, w_down_t)

        late = (GA_MOD, SB_MOD, CB_MOD, GB_MOD)
        wm_late = (v[1], kt[1], qt[1], r_den[1])
        late_bank = (sc[:, 0, :], sc[:, 1, :], num[:, :], kt_op[:, :])
        c_bc = k_tok[:, :].rearrange("p (k n) -> p k n", k=C)
        sign, size, gate, bo_row = (probs[:, i, :] for i in range(4))
        gb_row = bo_row

        def unit_of(u):
            return (u % 2, u // 2) if u < 2 * C else (2, u - 2 * C)

        block = s.enter_context(nc.Block())

        @block.sync
        def _(sp):
            def load_group(g):
                wait(sp, xt_ps, C * g)
                sp.dma_start(xg[:, :, :], x_groups[g, :, :, :] if isinstance(g, int) else
                             x_groups[bass.ds(g, 1), :, :, :].rearrange("a p t d -> (a p) t d")).then_inc(x_in, 16)

            def load_residual(tile, slot, uses):
                wait(sp, y_out[slot], 16 * uses)
                sp.dma_start(x_res[:, slot, :], x_tiles[tile, :, :] if isinstance(tile, int) else
                             x_tiles[bass.ds(tile, 1), :, :].rearrange("a p d -> (a p) d")).then_inc(xr_in[slot], 16)

            def store(tile, slot):
                wait(sp, y_ready, tile + 1)
                sp.dma_start(mid_tiles[tile, :, :] if isinstance(tile, int) else
                             mid_tiles[bass.ds(tile, 1), :, :].rearrange("a p d -> (a p) d"),
                             x_res[:, slot, :]).then_inc(y_out[slot], 16)

            def load_piece(i):
                if i == 0:
                    sp.wait_ge(xt_ps, (NG + 1) * C)
                elif i == 1:
                    sp.wait_ge(state_ready, (NG - 1) * GT)
                    sp.wait_ge(a_ready, (NG - 1) * GT)
                wait(sp, most_ready, i - RAW + 1)
                if i - RAW < 2 * C:
                    wait(sp, ffn_w_ready, i - RAW + 1)
                src = pieces[i]
                to = raw[i % RAW] if i < 2 * C else raw[i % RAW].rearrange("p (h n) -> p h n", h=3)
                sp.dma_start(to, src).then_inc(raw_in[i % RAW], 16)

            load_group(1)
            for i, m in enumerate(late):
                sp.dma_start(wm_late[i][:, :, :],
                             w_mod[:, m * D:(m + 1) * D].rearrange("(c p) n -> p c n", p=P)).then_inc(wm_late_in[i], 16)
                if i == 0:
                    sp.dma_start(bo_row, b_out.rearrange("(a n) -> a n", a=1).broadcast_to([P, D])).then_inc(bo_in, 16)
            sp.wait_ge(gb_ready, 1)
            sp.dma_start(gb_dram, gb_row[0:1, :]).then_inc(gb_saved, 16)

            def group(g, parity):
                if not isinstance(g, int) or g + 2 < NG:
                    load_group(g + 2)
                elif g + 2 == NG:
                    sp.wait_ge(y_out[0], 16 * GT // 2)
                    sp.wait_ge(y_out[1], 16 * GT // 2)
                    sp.wait_ge(xt_ps, C * NG)
                    sp.dma_start(xg[:, :, :], mid_groups[0, :, :, :]).then_inc(x_in, 16)
                last = isinstance(g, int) and g == NG - 1
                if last:
                    for i in range(RAW):
                        load_piece(i)
                for t in range(GT):
                    tile = g * GT + t
                    load_residual(tile, t % 2, g * 2 + t // 2)
                    if not isinstance(tile, int) or tile > 0:
                        store(tile - 1, (t + 1) % 2)
                    if last:
                        for i in ((), (5, 6), (7, 8, 9), (10, 11))[t]:
                            load_piece(i)

            groups(sp, 2, NG - 2, group)
            store(NG * GT - 1, 1)
            for slot in range(2):
                sp.wait_ge(y_out[slot], 16 * NG * GT // 2)

        @block.gpsimd
        def _(pool):
            def rstd_of(g):
                wait(pool, var_ready, g + 1)
                pool.tensor_tensor(out=rstd[:, :], in0=var_eps[:, :], in1=half_neg[:, :], op=ALU.pow).then_inc(rstd_ready, 1)

            def exp_part(g, n):
                wait(pool, exp_ready, g * 2 * C + n + 1)
                if not isinstance(g, int):
                    pool.sem_inc(pool_passed, 1)
                pool.tensor_scalar(z_exp[:, n % 2, :], z_exp[:, n % 2, :], 1.0, EPS_FEAT, ALU.min,
                                   ALU.add).then_inc(emin_ready, 1)

            def q_times_sum(g, parity, c):
                wait(pool, ksum_ready, g * C + c + 1)
                wait(pool, phi_ready, g * 2 * C + 2 * c + 2)
                wait(pool, prod_lo_ready, g * C + c)
                pool.tensor_tensor(out=prod[:, :], in0=k_sum[:, c % 2, :], in1=qt[parity][:, c, :],
                                   op=ALU.mult).then_inc(prod_ready, 1)

            def prod_low(g, c):
                wait(pool, prod_hi_ready, g * C + c + 1)
                pool.tensor_tensor(out=prod_lo[:, :], in0=prod[:, :], in1=prod_hi[:, :].bitcast(F32),
                                   op=ALU.subtract).then_inc(prod_lo_ready, 1)

            def a_low(tile):
                wait(pool, a_hi_ready, tile + 1)
                pool.tensor_tensor(out=a_lo[:, :], in0=a_t[:, :], in1=a_hi[:, :].bitcast(F32),
                                   op=ALU.subtract).then_inc(a_lo_ready, 1)

            def residual(tile, slot, uses):
                wait(pool, xr_in[slot], 16 * (uses + 1))
                pool.tensor_tensor(out=x_res[:, slot, :], in0=x_res[:, slot, :], in1=gabo_row[:, :],
                                   op=ALU.add).then_inc(xr_ready, 1)
                wait(pool, xr_ready, tile + 1)
                wait(pool, y_gated, tile + 1)
                pool.tensor_tensor(out=x_res[:, slot, :], in0=y[:, :], in1=x_res[:, slot, :],
                                   op=ALU.add).then_inc(y_ready, 1)

            def last_residual(g, t):
                tile = g * GT + t - 1
                if not isinstance(tile, int) or tile >= 0:
                    residual(tile, (t + 1) % 2, g * 2 + (t - 1) // 2)

            exp_part(0, 0)
            exp_part(0, 1)
            q_times_sum(0, 0, 0)
            exp_part(0, 2)
            prod_low(0, 0)
            exp_part(0, 3)
            q_times_sum(0, 0, 1)
            exp_part(0, 4)
            rstd_of(1)
            exp_part(0, 5)
            prod_low(0, 1)
            q_times_sum(0, 0, 2)
            exp_part(0, 6)
            exp_part(0, 7)
            prod_low(0, 2)
            q_times_sum(0, 0, 3)
            prod_low(0, 3)

            def group(g, parity):
                ahead = not isinstance(g, int) or g + 1 < NG
                two_ahead = not isinstance(g, int) or g + 2 <= NG
                n = g + 1
                other = 1 - parity
                if ahead:
                    exp_part(n, 0)
                last_residual(g, 0)
                if ahead:
                    exp_part(n, 1)
                if ahead:
                    q_times_sum(n, other, 0)
                a_low(g * GT)
                if ahead:
                    exp_part(n, 2)
                    prod_low(n, 0)
                    exp_part(n, 3)
                    exp_part(n, 4)
                    q_times_sum(n, other, 1)
                last_residual(g, 1)
                if ahead:
                    exp_part(n, 5)
                if ahead:
                    prod_low(n, 1)
                a_low(g * GT + 1)
                if ahead:
                    exp_part(n, 6)
                    exp_part(n, 7)
                    q_times_sum(n, other, 2)
                    prod_low(n, 2)
                if two_ahead:
                    rstd_of(g + 2)
                if ahead:
                    q_times_sum(n, other, 3)
                last_residual(g, 2)
                if ahead:
                    prod_low(n, 3)
                a_low(g * GT + 2)
                last_residual(g, 3)
                a_low(g * GT + 3)

            groups(pool, 2, NG - 2, group)
            residual(NG * GT - 1, 1, NG * 2 - 1)

        @block.scalar
        def _(act):
            def xt_high(g, c):
                wait(act, xf_ready, g * C + c + 1)
                act.activation(xt_hi[:, c, :], xf[:, c % 2, :], ACT.Copy).then_inc(xt_hi_done, 1)

            def exp_relu(g, n):
                kind, c = unit_of(n)
                bias, scale = qk_bias[:, 1 - kind, c:c + 1], (1.0, Q_SCALE)[kind]
                wait(act, pj_ready, g * UNITS + n + 1)
                wait(act, phi_ready, g * 2 * C + n - 1)
                act.activation(z_exp[:, n % 2, :], pj[:, n % 2, :], ACT.Exp, bias=bias, scale=scale).then_inc(exp_ready, 1)
                act.activation(z_relu[:, n % 2, :], pj[:, n % 2, :], ACT.Relu, bias=bias, scale=scale).then_inc(relu_ready, 1)

            def prod_high(g, c):
                wait(act, prod_ready, g * C + c + 1)
                wait(act, den_ps, g * C + c)
                act.activation(prod_hi[:, :], prod[:, :], ACT.Copy).then_inc(prod_hi_ready, 1)

            def den_out(g, parity, c):
                wait(act, den_ps, g * C + c + 1)
                act.activation(r_den[parity][:, c, :], den_tp[:, :], ACT.Copy, bias=EPS_DEN).then_inc(den_ready, 1)

            def spread_q(tile, g, parity, t):
                wait(act, phi_ready, (g + 1) * 2 * C)
                wait(act, sc_ready, (tile - 1) * C + SPLIT)
                for h in range(HPC):
                    rows = slice(h * E, (h + 1) * E)
                    ins = act.activation(q_diag[rows, :, h, :], qt[parity][rows, 0:SPLIT, t * P:(t + 1) * P], ACT.Copy)
                ins.then_inc(diag_ready, 1)

            def own_rows(tile, g, parity, t):
                cols = slice(t * P, (t + 1) * P)
                wait(act, phi_ready, (g + 1) * 2 * C)
                wait(act, sc_ready, tile * C)
                for p in range(2):
                    rows = slice(p * 64, (p + 1) * 64)
                    act.activation(k_pair[rows, :, p, :], kt[parity][rows, SPLIT:C, cols], ACT.Copy)
                for h in range(HPC):
                    rows = slice(h * E, (h + 1) * E)
                    ins = act.activation(q_high[rows, :, h, :], qt[parity][rows, SPLIT:C, cols], ACT.Copy)
                ins.then_inc(own_ready, 1)

            def other_rows(parity, t):
                for h in range(HPC):
                    rows, other = slice(h * E, (h + 1) * E), slice((h + 2) % HPC * E, (h + 2) % HPC * E + E)
                    ins = act.activation(q_high[other, :, h, :], qt[parity][rows, SPLIT:C, t * P:(t + 1) * P], ACT.Copy)
                ins.then_inc(other_ready, 1)

            def k_rows(tile):
                wait(act, kt_ps, tile + 1)
                wait(act, state_ready, tile)
                act.activation(k_tok[:, :], kt_op[:, :], ACT.Copy).then_inc(ktok_ready, 1)

            def state_out(tile):
                wait(act, state_ready, tile + 1)
                act.activation(kv_diag[:, :, :].rearrange("p c f -> p (c f)"), state[:, :], ACT.Copy).then_inc(kv_ready, 1)

            def a_high(tile):
                wait(act, a_ready, tile + 1)
                wait(act, op_ready, tile)
                act.activation(a_hi[:, :], a_t[:, :], ACT.Copy).then_inc(a_hi_ready, 1)

            def ffn_weights(t):
                for i in ((0, 1), (2, 3, 4), (5, 6, 7), ())[t]:
                    act.wait_ge(raw_in[i % RAW], 16 * (i // RAW + 1))
                    if i == 0:
                        act.wait_ge(pj_ready, NG * UNITS)
                    act.activation((w_hi if i < C else w_lo)[:, i % C, 0:HID], raw[i % RAW],
                                   ACT.Copy).then_inc(ffn_w_ready, 1)

            for c in range(C):
                xt_high(0, c)
            exp_relu(0, 0)
            exp_relu(0, 1)
            exp_relu(0, 2)
            prod_high(0, 0)
            exp_relu(0, 3)
            exp_relu(0, 4)
            exp_relu(0, 5)
            den_out(0, 0, 0)
            prod_high(0, 1)
            exp_relu(0, 6)
            exp_relu(0, 7)
            den_out(0, 0, 1)
            prod_high(0, 2)
            act.wait_ge(init_done, 1)
            own_rows(0, 0, 0, 0)
            spread_q(0, 0, 0, 0)
            other_rows(0, 0)
            den_out(0, 0, 2)
            prod_high(0, 3)
            den_out(0, 0, 3)
            for c in range(C):
                xt_high(1, c)

            def group(g, parity):
                ahead = not isinstance(g, int) or g + 1 < NG
                two_ahead = not isinstance(g, int) or g + 2 <= NG
                n = g + 1
                other = 1 - parity
                last = isinstance(g, int) and g == NG - 1
                if ahead:
                    exp_relu(n, 0)
                own_rows(g * GT + 1, g, parity, 1)
                spread_q(g * GT + 1, g, parity, 1)
                if ahead:
                    exp_relu(n, 1)
                k_rows(g * GT)
                other_rows(parity, 1)
                a_high(g * GT)
                if last:
                    ffn_weights(0)
                if ahead:
                    exp_relu(n, 2)
                state_out(g * GT)
                if ahead:
                    prod_high(n, 0)
                    exp_relu(n, 3)
                    exp_relu(n, 4)
                    den_out(n, other, 0)
                own_rows(g * GT + 2, g, parity, 2)
                spread_q(g * GT + 2, g, parity, 2)
                if ahead:
                    exp_relu(n, 5)
                    prod_high(n, 1)
                k_rows(g * GT + 1)
                other_rows(parity, 2)
                a_high(g * GT + 1)
                if last:
                    ffn_weights(1)
                if ahead:
                    exp_relu(n, 6)
                state_out(g * GT + 1)
                if ahead:
                    exp_relu(n, 7)
                    den_out(n, other, 1)
                    prod_high(n, 2)
                own_rows(g * GT + 3, g, parity, 3)
                spread_q(g * GT + 3, g, parity, 3)
                if ahead:
                    den_out(n, other, 2)
                    prod_high(n, 3)
                k_rows(g * GT + 2)
                other_rows(parity, 3)
                a_high(g * GT + 2)
                if last:
                    ffn_weights(2)
                state_out(g * GT + 2)
                if ahead:
                    den_out(n, other, 3)
                    spread_q(g * GT + 4, n, other, 0)
                if two_ahead:
                    xt_high(g + 2, 0)
                    xt_high(g + 2, 1)
                k_rows(g * GT + 3)
                if two_ahead:
                    xt_high(g + 2, 2)
                a_high(g * GT + 3)
                if last:
                    ffn_weights(3)
                if two_ahead:
                    xt_high(g + 2, 3)
                if ahead:
                    own_rows(g * GT + 4, n, other, 0)
                    other_rows(other, 0)
                state_out(g * GT + 3)

            groups(act, 2, NG - 2, group)

        @block.vector
        def _(dve):
            def norm_stats(g):
                wait(dve, x_in, 16 * (g + 1))
                for t in range(GT):
                    ins = dve.bn_stats(stats[:, t, :], xg[:, t, :])
                ins.then_inc(ln_chain, 1)

            def norm_var(g):
                wait(dve, ln_chain, 2 * g + 1)
                wait(dve, xn_ready, g)
                if not isinstance(g, int):
                    dve.sem_inc(dve_passed, 1)
                for t in range(GT):
                    ins = dve.bn_aggr(mean_var[:, t, :], stats[:, t, :])
                ins.then_inc(ln_chain, 1)
                wait(dve, ln_chain, 2 * g + 2)
                dve.tensor_scalar(var_eps[:, :], mean_var[:, :, 1], EPS_LN, None, ALU.add).then_inc(var_ready, 1)

            def norm_x(g):
                wait(dve, rstd_ready, g + 1)
                for t in range(GT):
                    ins = dve.tensor_scalar(xg[:, t, :], xg[:, t, :], mean_var[:, t, 0:1], rstd[:, t:t + 1],
                                            ALU.subtract, ALU.mult)
                ins.then_inc(xn_ready, 1)

            def xt_full(g, c):
                shift, scale = (SB, CB) if isinstance(g, int) and g == NG else (SA, CA)
                wait(dve, xt_ps, g * C + c + 1)
                if c < 2:
                    wait(dve, phi_ready, g * 2 * C)
                else:
                    wait(dve, xt_lo_done, g * C + c - 1)
                dve.tensor_scalar(xf[:, c % 2, :], turn_bank[c], mod_col[:, scale, c:c + 1],
                                  mod_col[:, shift, c:c + 1], ALU.mult, ALU.add).then_inc(xf_ready, 1)

            def xt_low(g, c):
                wait(dve, xt_hi_done, g * C + c + 1)
                dve.tensor_tensor(out=xt_lo[:, c, :], in0=xf[:, c % 2, :], in1=xt_hi[:, c, :].bitcast(F32),
                                  op=ALU.subtract).then_inc(xt_lo_done, 1)

            def x_by_feature(g):
                for c in range(C + 1):
                    if c < C:
                        xt_full(g, c)
                    if c > 0:
                        xt_low(g, c - 1)

            def feature(g, parity, n):
                kind, c = unit_of(n)
                to = (kt, qt)[kind][parity]
                wait(dve, emin_ready, g * 2 * C + n + 1)
                wait(dve, relu_ready, g * 2 * C + n + 1)
                dve.tensor_tensor(out=to[:, c, :], in0=z_exp[:, n % 2, :], in1=z_relu[:, n % 2, :],
                                  op=ALU.add).then_inc(phi_ready, 1)
                if kind == 0:
                    wait(dve, phi_ready, g * 2 * C + n + 1)
                    wait(dve, prod_ready, g * C + c - 1)
                    first = isinstance(g, int) and g == 0
                    wait(dve, past_ready, (g - 1) * C + c + 1)
                    dve.tensor_tensor_scan(k_sum[:, c % 2, :], to[:, c, :], to[:, c, :],
                                           0.0 if first else k_past[:, c:c + 1],
                                           ALU.add, ALU.bypass).then_inc(ksum_ready, 1)
                    wait(dve, ksum_ready, g * C + c + 1)
                    dve.tensor_copy(k_past[:, c:c + 1], k_sum[:, c % 2, GN - 1:GN]).then_inc(past_ready, 1)

            def v_rows(g, parity, t):
                wait(dve, pj_ready, g * UNITS + 2 * C + t + 1)
                dve.tensor_tensor(out=v[parity][:, t, :], in0=pj[:, t % 2, :], in1=bv_row[:, :],
                                  op=ALU.add).then_inc(v_ready, 1)

            def low_halves(tile, parity, t):
                cols = slice(t * P, (t + 1) * P)
                wait(dve, own_ready, tile + 1)
                for p in range(2):
                    rows, other = slice(p * 64, (p + 1) * 64), slice((1 - p) * 64, (2 - p) * 64)
                    dve.tensor_tensor(out=k_pair[other, :, p, :], in0=kt[parity][rows, SPLIT:C, cols],
                                      in1=k_pair[rows, :, p, :].bitcast(F32), op=ALU.subtract)
                for h in range(HPC):
                    rows = slice(h * E, (h + 1) * E)
                    ins = dve.tensor_tensor(out=q_low[rows, :, h, :], in0=qt[parity][rows, SPLIT:C, cols],
                                            in1=q_high[rows, :, h, :].bitcast(F32), op=ALU.subtract)
                ins.then_inc(low_ready, 1)

            def recip(g, parity, c):
                wait(dve, den_ready, g * C + c + 1)
                dve.reciprocal(r_den[parity][:, c, :], r_den[parity][:, c, :]).then_inc(rden_ready, 1)

            def mask(tile, c):
                wait(dve, sc_ready, tile * C + c + 1)
                dve.tensor_tensor(out=probs[:, c, :].rearrange("p (h i) -> p h i", h=HPC),
                                  in0=sc[:, c % 2, :].rearrange("p (h i) -> p h i", h=HPC),
                                  in1=causal[:, :].rearrange("p (a i) -> p a i", a=1).broadcast_to([P, HPC, P]),
                                  op=ALU.mult).then_inc(probs_ready, 1)

            def divide(tile, g, parity, t):
                wait(dve, num_ready, tile + 1)
                wait(dve, rden_ready, (g + 1) * C)
                wait(dve, a_lo_ready, tile)
                dve.tensor_tensor(out=a_t[:, :].rearrange("p (c i) -> p c i", c=C),
                                  in0=num[:, :].rearrange("p (c i) -> p c i", c=C),
                                  in1=r_den[parity][:, :, t * P:(t + 1) * P], op=ALU.mult).then_inc(a_ready, 1)

            def gate_y(tile):
                wait(dve, op_ready, tile + 1)
                wait(dve, y_ready, tile)
                dve.tensor_tensor(out=y[:, :], in0=kt_op[:, :], in1=ga_row[:, :],
                                  op=ALU.mult).then_inc(y_gated, 1)

            def gate_last(g, t):
                tile = g * GT + t - 1
                if not isinstance(tile, int) or tile >= 0:
                    gate_y(tile)

            def ffn_sizes(pieces):
                for i in pieces:
                    dve.wait_ge(raw_in[i % RAW], 16 * (i // RAW + 1))
                    dve.tensor_reduce(most[:, i:i + 1], raw[i % RAW], AX.X, ALU.max,
                                      apply_absolute_value=True).then_inc(most_ready, 1)

            chain = [0]

            def link(ins):
                chain[0] += 1
                ins.then_inc(late_chain, 1)
                dve.wait_ge(late_chain, chain[0])

            def gate_row(i, row):
                dve.wait_ge(late_mm, i + 1)
                link(dve.tensor_copy(gate, late_bank[i]))
                link(dve.tensor_scalar(sign, gate, 0.0, 2.0, ALU.is_ge, ALU.mult))
                link(dve.tensor_scalar(sign, sign, -1.0, None, ALU.add))
                link(dve.tensor_scalar(size, gate, -1.0, 0.25, ALU.mult, ALU.max))
                link(dve.tensor_tensor(out=size, in0=size, in1=gate, op=ALU.max))
                link(dve.tensor_tensor(out=row, in0=sign, in1=size, op=ALU.mult))

            x_by_feature(0)
            dve.memset(ones[:, :], 1.0)
            link(dve.memset(kv_diag[:, :, :], 0.0))
            zeros = kv_diag[:, :, :].rearrange("p (a c) f -> p a (c f)", a=1).broadcast_to([P, SPLIT, D])
            dve.tensor_copy(q_diag[:, :, :, :].rearrange("p c h i -> p c (h i)"), zeros)
            dve.tensor_copy(q_high[:, :, :, :].rearrange("p c h i -> p c (h i)"), zeros)
            dve.tensor_copy(q_low[:, :, :, :].rearrange("p c h i -> p c (h i)"), zeros).then_inc(init_done, 1)
            for k in range(C):
                ins = dve.tensor_scalar(c_bc[:, k, :], causal[:, :], 0.0, c_col[:, k:k + 1], ALU.mult, ALU.add)
            ins.then_inc(c_bc_ready, 1)
            for n in range(4):
                feature(0, 0, n)
            norm_stats(1)
            norm_var(1)
            feature(0, 0, 4)
            gate_row(0, ga_row[:, :])
            feature(0, 0, 5)
            dve.wait_ge(bo_in, 16)
            link(dve.tensor_tensor(out=gabo_row[:, :], in0=ga_row[:, :], in1=bo_row, op=ALU.mult))
            norm_x(1)
            feature(0, 0, 6)
            gate_row(3, gb_row)
            dve.tensor_scalar(gb_row, gb_row, W_SCALE, W_SCALE, ALU.mult, ALU.mult).then_inc(gb_ready, 1)
            dve.tensor_copy(mod_col[:, SB, :], late_bank[1][:, 0:C])
            dve.tensor_scalar(mod_col[:, CB, :], late_bank[2][:, 0:C], 1.0, None, ALU.add)
            feature(0, 0, 7)
            v_rows(0, 0, 0)
            recip(0, 0, 0)
            v_rows(0, 0, 1)
            v_rows(0, 0, 2)
            recip(0, 0, 1)
            v_rows(0, 0, 3)
            x_by_feature(1)
            dve.wait_ge(gb_saved, 16)

            def group(g, parity):
                ahead = not isinstance(g, int) or g + 1 < NG
                two_ahead = not isinstance(g, int) or g + 2 <= NG
                n = g + 1
                other = 1 - parity
                last = isinstance(g, int) and g == NG - 1
                for t in range(GT):
                    tile = g * GT + t
                    mask(tile, 0)
                    mask(tile, 1)
                    low_halves(tile, parity, t)
                    if t == 0:
                        recip(g, parity, 2)
                    elif t == 1 and ahead:
                        feature(n, other, 3)
                    elif t == 2 and ahead:
                        feature(n, other, 7)
                    elif ahead:
                        v_rows(n, other, 3)
                    gate_last(g, t)
                    mask(tile, 2)
                    mask(tile, 3)
                    if ahead and t < 2:
                        feature(n, other, 4 * t)
                    elif ahead and t == 2:
                        v_rows(n, other, 0)
                    elif two_ahead and t == 3:
                        xt_full(g + 2, 0)
                        xt_full(g + 2, 1)
                    if t == 0:
                        recip(g, parity, 3)
                    elif t == 1 and ahead:
                        recip(n, other, 0)
                    elif t == 2 and ahead:
                        recip(n, other, 1)
                    if ahead and t < 2:
                        feature(n, other, 4 * t + 1)
                    elif ahead and t == 2:
                        v_rows(n, other, 1)
                    elif two_ahead and t == 3:
                        xt_low(g + 2, 0)
                        xt_full(g + 2, 2)
                        xt_low(g + 2, 1)
                    if last:
                        ffn_sizes(((0,), (2, 3), (5, 6), (8, 9))[t])
                    divide(tile, g, parity, t)
                    if two_ahead and t == 3:
                        xt_full(g + 2, 3)
                        xt_low(g + 2, 2)
                    if two_ahead and t == 1:
                        norm_stats(g + 2)
                        norm_var(g + 2)
                    if ahead and t < 2:
                        feature(n, other, 4 * t + 2)
                    elif ahead and t == 2:
                        v_rows(n, other, 2)
                    elif two_ahead and t == 3:
                        xt_low(g + 2, 3)
                    if two_ahead and t == 2:
                        norm_x(g + 2)
                    if last:
                        ffn_sizes(((1,), (4,), (7,), (10, 11))[t])

            groups(dve, 2, NG - 2, group)
            dve.wait_ge(most_ready, 3 * C)
            dve.tensor_reduce(beyond[:, :], most[:, :], AX.X, ALU.max).then_inc(beyond_ready, 1)
            dve.wait_ge(beyond_ready, 1)
            dve.tensor_scalar(beyond[:, :], beyond[:, :], EXACT, None, ALU.is_gt).then_inc(beyond_ready, 1)
            gate_y(NG * GT - 1)
            dve.wait_ge(beyond_ps, 1)
            dve.tensor_scalar(wide[:, :], pj[0:1, 0, 0:1], 0.5, None, ALU.is_gt).then_inc(wide_ready, 1)
            dve.wait_ge(wide_ready, 1)

        @block.tensor
        def _(pe):
            def x_turn(g, c):
                wait(pe, xn_ready, g + 1)
                if c == 0:
                    wait(pe, v_ready, (g - 1) * C + 3)
                elif c == 1:
                    wait(pe, den_ready, g * C)
                elif c == 2:
                    wait(pe, v_ready, g * C)
                else:
                    wait(pe, xf_ready, g * C + 2)
                for t in range(GT):
                    mm = pe.transpose(turn_bank[c][:, t * P:(t + 1) * P], xg[:, t, c * P:(c + 1) * P], ident[:, :])
                mm.then_inc(xt_ps, 1)

            def project(g, u):
                kind, c = unit_of(u)
                if u == 0:
                    wait(pe, xt_lo_done, (g + 1) * C)
                if u < 2:
                    pass
                elif u < 2 * C + 2:
                    wait(pe, relu_ready, g * 2 * C + u - 1)
                else:
                    wait(pe, v_ready, g * C + u - 2 * C - 1)
                to = pj[:, u % 2, :]
                passes = [(hi_w, hi_x, k) for hi_w, hi_x in ((1, 1), (1, 0), (0, 1)) for k in range(C)]
                for i, (hi_w, hi_x, k) in enumerate(passes):
                    w = w_hi if hi_w else w_lo
                    xt = xt_hi if hi_x else xt_lo
                    if kind == 2:
                        mm = pe.matmul(to, xt[:, k, c * P:(c + 1) * P], w[:, k, WV:WV + D],
                                       start=(i == 0), stop=(i == len(passes) - 1))
                    else:
                        at = (WK, WQ)[kind] + c * P
                        mm = pe.matmul(to, w[:, k, at:at + P], xt[:, k, :],
                                       start=(i == 0), stop=(i == len(passes) - 1))
                mm.then_inc(pj_ready, 1)

            def denominators(g, c):
                wait(pe, prod_lo_ready, g * C + c + 1)
                if c == 0:
                    wait(pe, xf_ready, (g + 1) * C)
                else:
                    wait(pe, den_ready, g * C + c)
                pe.matmul(den_tp[:, :], head_ones[:, :], prod_hi[:, :], start=True, stop=False)
                pe.matmul(den_tp[:, :], head_ones[:, :], prod_lo[:, :], start=False, stop=True).then_inc(den_ps, 1)

            def scores(tile, parity, t, c):
                if c == 0:
                    wait(pe, diag_ready, tile + 1)
                elif c == SPLIT:
                    wait(pe, other_ready, tile + 1)
                    wait(pe, low_ready, tile + 1)
                wait(pe, probs_ready, tile * C + c - 1)
                if c < SPLIT:
                    mm = pe.matmul(sc[:, c % 2, :], kt[parity][:, c, t * P:(t + 1) * P],
                                   q_diag[:, c, :, :].rearrange("p h i -> p (h i)"), start=True, stop=True)
                else:
                    for p in range(2):
                        to = sc[:, c % 2, p * 2 * P:(p + 1) * 2 * P]
                        for half in (q_high, q_low):
                            mm = pe.matmul(to, k_pair[:, c - SPLIT, p, :],
                                           half[:, c - SPLIT, 2 * p:2 * p + 2, :].rearrange("p h i -> p (h i)"),
                                           start=(half is q_high), stop=(half is q_low))
                mm.then_inc(sc_ready, 1)

            def k_turn(tile, parity, t):
                wait(pe, y_gated, tile)
                for c in range(C):
                    mm = pe.transpose(kt_op[:, c * P:(c + 1) * P], kt[parity][:, c, t * P:(t + 1) * P], ident[:, :])
                mm.then_inc(kt_ps, 1)

            def numerators(tile, g, parity, t):
                wait(pe, kv_ready, tile)
                wait(pe, a_ready, tile)
                for c in range(C):
                    pe.matmul(num[:, c * P:(c + 1) * P], kv_diag[:, c, :], qt[parity][:, c, t * P:(t + 1) * P],
                              start=(c == 0), stop=False, skip_group_check=True)
                wait(pe, v_ready, g * C + t + 1)
                for c in range(C):
                    wait(pe, probs_ready, tile * C + c + 1)
                    for h in range(HPC):
                        f = c * P + h * E
                        mm = pe.matmul(num[h * E:(h + 1) * E, c * P:(c + 1) * P], v[parity][:, t, f:f + E],
                                       probs[:, c, h * P:(h + 1) * P], start=False, stop=(c == C - 1),
                                       skip_group_check=True)
                mm.then_inc(num_ready, 1)

            def add_state(tile, parity, t):
                wait(pe, ktok_ready, tile + 1)
                for c in range(C):
                    for h in range(HPC):
                        f = slice(c * P + h * E, c * P + (h + 1) * E)
                        mm = pe.matmul(state[h * E:(h + 1) * E, f], k_tok[:, f], v[parity][:, t, f],
                                       start=False, stop=False, skip_group_check=True)
                mm.then_inc(state_ready, 1)

            def out_project(tile):
                wait(pe, a_lo_ready, tile + 1)
                wait(pe, ktok_ready, tile + 1)
                passes = [(a, w, c) for a, w in ((a_hi, w_hi), (a_hi, w_lo), (a_lo, w_hi)) for c in range(C)]
                for i, (a, w, c) in enumerate(passes):
                    mm = pe.matmul(kt_op[:, :], a[:, c * P:(c + 1) * P], w[:, c, WO:WO + D],
                                   start=(i == 0), stop=(i == len(passes) - 1))
                mm.then_inc(op_ready, 1)

            def modulation(i):
                pe.wait_ge(wm_late_in[i], 16)
                if i in (0, 3):
                    pe.wait_ge(c_bc_ready, 1)
                    for k in range(C):
                        mm = pe.matmul(late_bank[i], c_bc[:, k, :], wm_late[i][:, k, :],
                                       start=(k == 0), stop=(k == C - 1))
                else:
                    mm = modulation_column(pe, late_bank[i], wm_late[i], c_col)
                mm.then_inc(late_mm, 1)

            for c in range(C):
                x_turn(0, c)
            for u in range(UNITS):
                project(0, u)
                if u == 2:
                    pe.wait_ge(init_done, 1)
                    pe.matmul(state[:, :], kv_diag[:, 0, :], kv_diag[:, :, :].rearrange("p c f -> p (c f)"),
                              start=True, stop=False, skip_group_check=True)
                if 3 <= u < 7:
                    modulation(u - 3)
                if u in (5, 7, 9, 11):
                    denominators(0, (u - 5) // 2)
            for c in range(C):
                x_turn(1, c)

            def group(g, parity):
                ahead = not isinstance(g, int) or g + 1 < NG
                two_ahead = not isinstance(g, int) or g + 2 <= NG
                n = g + 1
                for t in range(GT):
                    tile = g * GT + t

                    def fill(i):
                        if 4 * t + i < UNITS - 1 and ahead:
                            project(n, 4 * t + i)
                        elif t == 3:
                            if i == 0 and ahead:
                                project(n, UNITS - 1)
                            if two_ahead:
                                for c in ((), (0, 1, 2), (3,), ())[i]:
                                    x_turn(g + 2, c)

                    scores(tile, parity, t, 0)
                    scores(tile, parity, t, 1)
                    if t == 0 and (not isinstance(tile, int) or tile > 0):
                        out_project(tile - 1)
                    fill(0)
                    if t == 1 and ahead:
                        denominators(n, 0)
                    if t > 0:
                        out_project(tile - 1)
                    scores(tile, parity, t, 2)
                    scores(tile, parity, t, 3)
                    fill(1)
                    if t == 2 and ahead:
                        denominators(n, 2)
                    k_turn(tile, parity, t)
                    numerators(tile, g, parity, t)
                    fill(2)
                    if t == 1 and ahead:
                        denominators(n, 1)
                    add_state(tile, parity, t)
                    fill(3)
                    if t == 2 and ahead:
                        denominators(n, 3)

            groups(pe, 2, NG - 2, group)
            out_project(NG * GT - 1)
            pe.wait_ge(beyond_ready, 2)
            pe.matmul(pj[0:1, 0, 0:1], beyond[:, :], ones[:, :], start=True, stop=True).then_inc(beyond_ps, 1)


def feed_forward(nc, sem, sbuf, psum, ident, mod_col, half_neg, w_hi, w_lo, xt_hi0, xt_lo0, wide, gb_dram,
                 w_gate_t, w_up_t, w_down_t, x_mid, out):
    with ExitStack() as s:
        xg = [sbuf(s, f"fx{i}", [P, GT, D]) for i in range(2)]
        xn = sbuf(s, "fxn", [P, GT, D])
        stats = sbuf(s, "fstats", [P, GT, 6])
        mean_var = sbuf(s, "fmean_var", [P, GT, 2])
        var_eps = sbuf(s, "fvar_eps", [P, GT])
        rstd = sbuf(s, "frstd", [P, GT])
        xt_hi = [xt_hi0, sbuf(s, "fxt_hi1", [P, C, GN], F32R)]
        xt_lo = [xt_lo0, sbuf(s, "fxt_lo1", [P, C, GN], F32R)]
        xf = sbuf(s, "fxf", [P, 2, GN])
        wg, wu = w_hi, w_lo
        wd = sbuf(s, "wd", [P, HB, D], F32R)
        gb_row = sbuf(s, "gb_row", [P, D])
        gate = sbuf(s, "gate", [P, 2, GN])
        h = sbuf(s, "h", [P, 2, GN])
        h_hi = sbuf(s, "h_hi", [P, HB, GN], F32R)
        h_lo = sbuf(s, "h_lo", [P, HB, GN], F32R)
        y = sbuf(s, "fy", [P, 2, D])
        gu = psum(s, "gu", [P, 4, 512])
        tp = psum(s, "tp", [P, 2, 512])
        dn = psum(s, "dn", [P, 2, 512])

        x_in, y_out = [sem(f"fx_in{i}") for i in range(2)], [sem(f"fy_out{i}") for i in range(2)]
        ln_chain, var_ready, rstd_ready, xn_ready = (sem("fln_chain"), sem("fvar_ready"), sem("frstd_ready"),
                                                     sem("fxn_ready"))
        xt_ps, xf_ready, xt_hi_done, xt_lo_done = sem("fxt_ps"), sem("fxf_ready"), sem("fxt_hi_done"), sem("fxt_lo_done")
        down_in, wd_ready = [sem(f"down_in{i}") for i in range(2)], sem("wd_ready")
        gb_in, int_in, word_ready, w_moved = sem("gb_in"), sem("int_in"), sem("word_ready"), sem("w_moved")
        gate_ps, up_ps, gate_ready, h_ready, h_hi_ready, h_lo_ready = (
            sem("gate_ps"), sem("up_ps"), sem("gate_ready"), sem("h_ready"), sem("h_hi_ready"), sem("h_lo_ready"))
        dn_ps, y_gated, y_ready, dve_passed = sem("dn_ps"), sem("fy_gated"), sem("fy_ready"), sem("fdve_passed")

        mid_groups = x_mid.rearrange("(g t p) d -> g p t d", t=GT, p=P)
        out_tiles = out.rearrange("a (t p) d -> (a t) p d", p=P)

        down_chunks = w_down_t.rearrange("(j p) n -> j p n", p=P)
        down_raw = [y[:, i, :].bitcast(I32) for i in range(2)]

        block = s.enter_context(nc.Block())

        @block.sync
        def _(sp):
            def load(g, parity):
                wait(sp, y_ready, (g - 1) * GT)
                sp.dma_start(xg[parity][:, :, :], mid_groups[g, :, :, :] if isinstance(g, int) else
                             mid_groups[bass.ds(g, 1), :, :, :].rearrange("a p t d -> (a p) t d")).then_inc(x_in[parity], 16)

            sp.dma_start(gb_row[:, :], gb_dram.broadcast_to([P, D])).then_inc(gb_in, 16)
            for j in range(HB):
                wait(sp, wd_ready, j - 1)
                sp.dma_start(down_raw[j % 2], down_chunks[j, :, :]).then_inc(down_in[j % 2], 16)
                if j == 1:
                    load(1, 1)
            load(0, 0)

            def group(g, parity):
                if isinstance(g, int) and g == 0:
                    pass
                elif not isinstance(g, int) or g + 1 < NG:
                    load(g + 1, 1 - parity)
                for t in range(GT):
                    tile = g * GT + t
                    wait(sp, y_ready, tile + 1)
                    sp.dma_start(out_tiles[tile, :, :] if isinstance(tile, int) else
                                 out_tiles[bass.ds(tile, 1), :, :].rearrange("a p d -> (a p) d"),
                                 y[:, t % 2, :]).then_inc(y_out[t % 2], 16)

            groups(sp, 2, NG - 2, group)
            for slot in range(2):
                sp.wait_ge(y_out[slot], 16 * NG * GT // 2)

        @block.gpsimd
        def _(pool):
            def rstd_of(g):
                wait(pool, var_ready, g)
                pool.tensor_tensor(out=rstd[:, :], in0=var_eps[:, :], in1=half_neg[:, :], op=ALU.pow).then_inc(rstd_ready, 1)

            def h_low(g, j):
                wait(pool, h_hi_ready, g * HB + j + 1)
                pool.tensor_tensor(out=h_lo[:, j, :], in0=h[:, j % 2, :], in1=h_hi[:, j, :].bitcast(F32),
                                   op=ALU.subtract).then_inc(h_lo_ready, 1)

            def group(g, parity):
                for j in range(HB):
                    h_low(g, j)
                    if j == 1 and (not isinstance(g, int) or g + 1 < NG):
                        rstd_of(g + 1)
                if isinstance(g, int) and g == 0:
                    pool.wait_ge(x_in[0], 16)
                for t in range(GT):
                    wait(pool, y_gated, g * GT + t + 1)
                    pool.tensor_tensor(out=y[:, t % 2, :], in0=y[:, t % 2, :], in1=xg[parity][:, t, :],
                                       op=ALU.add).then_inc(y_ready, 1)

            groups(pool, 2, NG - 2, group)

        def words(act, src, to, done):
            act.dma_start(h[:, 0, :].bitcast(I32), src).then_inc(int_in, 16)
            act.wait_ge(int_in, 16 * (done + 1))
            act.activation(gate[:, 0, :], h[:, 0, :].bitcast(I32), ACT.Copy).then_inc(word_ready, 1)
            act.wait_ge(word_ready, done + 1)
            act.dma_start(to.bitcast(F32), gate[:, 0, :]).then_inc(w_moved, 16)
            act.wait_ge(w_moved, 16 * (done + 1))

        @block.scalar
        def _(act):
            def xt_high(g, parity, c):
                wait(act, xt_ps, (g - 1) * C + c + 1)
                wait(act, xt_lo_done, (g - 1) * C + c - 1)
                act.activation(xf[:, c % 2, :], tp[:, c % 2, :], ACT.Identity, bias=mod_col[:, SB, c:c + 1],
                               scale=mod_col[:, CB, c:c + 1]).then_inc(xf_ready, 1)
                wait(act, xf_ready, (g - 1) * C + c + 1)
                act.activation(xt_hi[parity][:, c, :], xf[:, c % 2, :], ACT.Copy).then_inc(xt_hi_done, 1)

            flag = act.value_load(wide[0:1, 0:1])
            with act.If(flag > 0):
                done = 0
                for w, src in ((wg, w_gate_t), (wu, w_up_t)):
                    for k in range(C):
                        for b in range(HID // D):
                            cols = slice(b * D, (b + 1) * D)
                            words(act, src[k * P:(k + 1) * P, cols], w[:, k, cols], done)
                            done += 1
                for j in range(HB):
                    act.wait_ge(down_in[j % 2], 16 * (j // 2 + 1))
                    act.activation(gate[:, 0, :], down_raw[j % 2], ACT.Copy).then_inc(word_ready, 1)
                    done += 1
                    act.wait_ge(word_ready, done)
                    act.dma_start(wd[:, j, :].bitcast(F32), gate[:, 0, :]).then_inc(w_moved, 16)
                    act.wait_ge(w_moved, 16 * done)
                    act.sem_inc(wd_ready, 1)

            def down_weights(js):
                with act.If(flag < 1):
                    for j in js:
                        act.wait_ge(down_in[j % 2], 16 * (j // 2 + 1))
                        act.activation(wd[:, j, :], down_raw[j % 2], ACT.Copy).then_inc(wd_ready, 1)

            def group(g, parity):
                for j in range(HB):
                    n = g * HB + j
                    wait(act, gate_ps, n + 1)
                    wait(act, h_ready, n - 1)
                    act.activation(gate[:, j % 2, :], gu[:, 2 * (j % 2), :], ACT.Silu,
                                   scale=W_SCALE).then_inc(gate_ready, 1)
                    wait(act, h_ready, n + 1)
                    act.activation(h_hi[:, j, :], h[:, j % 2, :], ACT.Copy).then_inc(h_hi_ready, 1)
                    if isinstance(g, int) and g == 0 and j < HB // 2:
                        down_weights((2 * j, 2 * j + 1))
                    if j >= 4 and j < 8 and (not isinstance(g, int) or g + 1 < NG):
                        xt_high(g + 1, 1 - parity, j - 4)

            groups(act, 2, NG - 2, group)

        @block.vector
        def _(dve):
            def norm_stats(g, parity):
                wait(dve, x_in[parity], 16 * (g // 2 + 1) if isinstance(g, int) else g * 8 + (16 - 8 * parity))
                wait(dve, ln_chain, 2 * (g - 1))
                for t in range(GT):
                    ins = dve.bn_stats(stats[:, t, :], xg[parity][:, t, :])
                ins.then_inc(ln_chain, 1)
                wait(dve, ln_chain, 2 * (g - 1) + 1)
                wait(dve, xn_ready, g - 1)
                if not isinstance(g, int):
                    dve.sem_inc(dve_passed, 1)
                for t in range(GT):
                    ins = dve.bn_aggr(mean_var[:, t, :], stats[:, t, :])
                ins.then_inc(ln_chain, 1)
                wait(dve, ln_chain, 2 * g)
                dve.tensor_scalar(var_eps[:, :], mean_var[:, :, 1], EPS_LN, None, ALU.add).then_inc(var_ready, 1)

            def norm_x(g, parity):
                wait(dve, rstd_ready, g)
                wait(dve, xt_ps, (g - 1) * C)
                for t in range(GT):
                    ins = dve.tensor_scalar(xn[:, t, :], xg[parity][:, t, :], mean_var[:, t, 0:1], rstd[:, t:t + 1],
                                            ALU.subtract, ALU.mult)
                ins.then_inc(xn_ready, 1)

            def xt_low(g, parity, c):
                wait(dve, xt_hi_done, (g - 1) * C + c + 1)
                dve.tensor_tensor(out=xt_lo[parity][:, c, :], in0=xf[:, c % 2, :], in1=xt_hi[parity][:, c, :].bitcast(F32),
                                  op=ALU.subtract).then_inc(xt_lo_done, 1)

            def group(g, parity):
                ahead = not isinstance(g, int) or g + 1 < NG
                for j in range(HB):
                    n = g * HB + j
                    wait(dve, up_ps, n + 1)
                    wait(dve, gate_ready, n + 1)
                    wait(dve, h_lo_ready, n - 1)
                    dve.tensor_tensor(out=h[:, j % 2, :], in0=gu[:, 2 * (j % 2) + 1, :], in1=gate[:, j % 2, :],
                                      op=ALU.mult).then_inc(h_ready, 1)
                    if ahead and j == 0:
                        norm_stats(g + 1, 1 - parity)
                    if ahead and j == 2:
                        norm_x(g + 1, 1 - parity)
                    if ahead and 4 <= j < 8:
                        xt_low(g + 1, 1 - parity, j - 4)
                for t in range(GT):
                    if isinstance(g, int) and g == 0 and t == 0:
                        dve.wait_ge(gb_in, 16)
                    wait(dve, dn_ps, g * GT + t + 1)
                    wait(dve, y_out[t % 2], g * 32 + 16 * (t // 2))
                    dve.tensor_tensor(out=y[:, t % 2, :], in0=dn[:, t % 2, :], in1=gb_row[:, :],
                                      op=ALU.mult).then_inc(y_gated, 1)

            groups(dve, 2, NG - 2, group)

        @block.tensor
        def _(pe):
            def x_turn(g, c):
                wait(pe, xn_ready, g)
                wait(pe, xf_ready, (g - 1) * C + c - 1)
                for t in range(GT):
                    mm = pe.transpose(tp[:, c % 2, t * P:(t + 1) * P], xn[:, t, c * P:(c + 1) * P], ident[:, :])
                mm.then_inc(xt_ps, 1)

            def passes(exact):
                return (lambda ap: ap) if exact else (lambda ap: ap.bitcast(F32))

            def all_groups(exact):
                as_ = passes(exact)

                def hidden(g, parity, j, w, bank, done):
                    for i, (xt, k) in enumerate((xt, k) for xt in (xt_hi, xt_lo) for k in range(C)):
                        mm = pe.matmul(gu[:, bank, :], as_(w[:, k, j * P:(j + 1) * P]), as_(xt[parity][:, k, :]),
                                       start=(i == 0), stop=(i == 2 * C - 1))
                    mm.then_inc(done, 1)

                def down(g, t):
                    wait(pe, y_gated, g * GT + t - 1)
                    for j in range(HB):
                        if t == 0:
                            wait(pe, h_lo_ready, g * HB + j + 1)
                            if isinstance(g, int) and g == 0:
                                pe.wait_ge(wd_ready, j + 1)
                        for half in (h_hi, h_lo):
                            mm = pe.matmul(dn[:, t % 2, :], as_(half[:, j, t * P:(t + 1) * P]), as_(wd[:, j, :]),
                                           start=(j == 0 and half is h_hi), stop=(j == HB - 1 and half is h_lo))
                    mm.then_inc(dn_ps, 1)

                def group(g, parity):
                    wait(pe, xt_lo_done, g * C)
                    for j in range(HB):
                        n = g * HB + j
                        wait(pe, gate_ready, n - 1)
                        hidden(g, parity, j, wg, 2 * (j % 2), gate_ps)
                        wait(pe, h_ready, n - 1)
                        hidden(g, parity, j, wu, 2 * (j % 2) + 1, up_ps)
                        if 4 <= j < 8 and (not isinstance(g, int) or g + 1 < NG):
                            x_turn(g + 1, j - 4)
                    for t in range(GT):
                        down(g, t)

                groups(pe, 2, NG - 2, group)

            flag = pe.value_load(wide[0:1, 0:1])
            with pe.If(flag > 0):
                pe.wait_ge(w_moved, 16 * 3 * HB)
                all_groups(False)
            with pe.Else():
                all_groups(True)


_INS = ["L0_attn_x", "L0_attn_W_qkv", "L0_attn_b_qkv", "L0_attn_W_out", "L0_attn_b_out",
        "L0_ffn_w_gate", "L0_ffn_w_up", "L0_ffn_w_down", "L0_c", "L0_wmod"]
_TURNED = ("L0_ffn_w_gate", "L0_ffn_w_up", "L0_ffn_w_down", "L0_c")


def kernel(**inputs):
    import concourse.bacc as bacc
    from concourse.bass_utils import run_bass_kernel_spmd

    nc = bacc.Bacc("TRN2", target_bir_lowering=False, num_devices=1, dynamic_dma_scratch_size=1024)
    arrays, args = {}, []
    for name in _INS:
        a = np.asarray(inputs[name])
        if name == "L0_c":
            a = a.reshape(C, P)
        layouts = [(f"in_{name}", a.T if name in _TURNED else a)]
        if name == "L0_attn_b_qkv":
            layouts.append(("in_b_cols", a.reshape(3 * C, P).T))
        for label, a in layouts:
            arrays[label] = np.ascontiguousarray(a)
            args.append(nc.dram_tensor(label, a.shape, mybir.dt.from_np(a.dtype), kind="ExternalInput").ap())
    out = nc.dram_tensor("out", (1, L, D), F32, kind="ExternalOutput").ap()
    build(nc, *args, out)
    r = run_bass_kernel_spmd(nc, [arrays], core_ids=[0])
    return r.results[0]["out"]
```
